# Optimizing a Trainium2 kernel written in Bass

```python
import numpy as np
import jax
import jax.numpy as jnp

def _softmax(x, axis=-1):
    return jax.nn.softmax(x, axis=axis)

def _gelu(x):
    return jax.nn.gelu(x, approximate=True)

def _silu(x):
    return jax.nn.silu(x)

def _sigmoid(x):
    return jax.nn.sigmoid(x)

def _layernorm(x, axis=-1, eps=1e-05):
    m = jnp.mean(x, axis=axis, keepdims=True)
    v = jnp.var(x, axis=axis, keepdims=True)
    return (x - m) / jnp.sqrt(v + eps)

def _scatter_add(tgt, idx, src, axis=0):
    return tgt.at[idx].add(src)

def _segment_sum(src, seg, n):
    return jax.ops.segment_sum(src, seg, n)
kernel_name = 'mk_flamingo_gated_d1_seqx_r8_c3305a'

def setup_inputs(seed: int=0):
    np.random.seed(seed)
    _w = jnp.asarray

    def _rec_inputs():
        import jax
        import jax.numpy as jnp
        _rk = jax.random.key(seed)
        x = 4.136e-05 + 0.9999 * jax.random.normal(jax.random.fold_in(_rk, 1), (4, 256, 256), jnp.float32)
        _lenS = 256 - jax.random.randint(jax.random.fold_in(_rk, 7), (4,), 0, max(1, 256 // 4) + 1, jnp.int32)
        _lenS2 = 256 - jax.random.randint(jax.random.fold_in(_rk, 8), (4,), 0, max(1, 256 // 4) + 1, jnp.int32)
        _ctx_1024P = jax.random.normal(jax.random.fold_in(_rk, 11), (4, 16, 128), jnp.float32)
        _ctx_1024c = jax.random.dirichlet(jax.random.fold_in(_rk, 511), 0.3 * jnp.ones((16,), jnp.float32), (4, 256))
        _ctx_1024t = jnp.einsum('bsk,bkd->bsd', _ctx_1024c, _ctx_1024P)
        _ctx_1024t = _ctx_1024t * jax.lax.rsqrt(jnp.mean(jnp.square(_ctx_1024t)) + 1e-12) * 0.953939
        ctx_1024 = -0.000292821 + 1.00034 * (_ctx_1024t + 0.3 * jax.random.normal(jax.random.fold_in(_rk, 611), (4, 256, 128), jnp.float32))
        _g = jax.random.normal(jax.random.fold_in(_rk, 9001), (2, 1), jnp.float32)
        _g = jnp.sign(_g) * jnp.maximum(jnp.abs(_g), 1.0) + (_g == 0) * 1.0
        g_xattn = _g[0]
        g_ffn = _g[1]
        return (x, ctx_1024, g_xattn, g_ffn)
    x, ctx_1024, g_xattn, g_ffn = _rec_inputs()

    def _L0_xattn_setup():
        import jax, jax.numpy as jnp
        import numpy as np
        import math
        B, L, DM = (2, 256, 128)
        DS, DC, EXP = (16, 4, 2)
        DI = EXP * DM
        DR = math.ceil(DM / 16)
        DT_MIN, DT_MAX, DT_FLOOR = (0.001, 0.1, 0.0001)

        def _ssm_forward(hidden_states, z, in_proj_w, conv_w, conv_b, x_proj_w, dt_proj_w, dt_proj_b, A_log, D):
            b = hidden_states.shape[0]
            x = jnp.einsum('ed,bld->bel', in_proj_w, hidden_states)
            xp = jnp.pad(x, ((0, 0), (0, 0), (DC - 1, 0)))
            xc = jax.lax.conv_general_dilated(xp, conv_w[:, None, :], window_strides=(1,), padding='VALID', dimension_numbers=('NCH', 'OIH', 'NCH'), feature_group_count=DI)
            u = jax.nn.silu(xc + conv_b[None, :, None])
            x_dbl = jnp.einsum('ke,bel->bkl', x_proj_w, u)
            dt_lo = x_dbl[:, :DR]
            Bm = x_dbl[:, DR:DR + DS]
            Cm = x_dbl[:, DR + DS:]
            delta = jax.nn.softplus(jnp.einsum('er,brl->bel', dt_proj_w, dt_lo) + dt_proj_b[None, :, None])
            A = -jnp.exp(A_log)

            def step(state, xs):
                d_t, B_t, C_t, u_t = xs
                dA = jnp.exp(d_t[..., None] * A)
                state = state * dA + (d_t * u_t)[..., None] * B_t[:, None, :]
                y_t = jnp.einsum('ben,bn->be', state, C_t)
                return (state, y_t)
            xs = (jnp.moveaxis(delta, -1, 0), jnp.moveaxis(Bm, -1, 0), jnp.moveaxis(Cm, -1, 0), jnp.moveaxis(u, -1, 0))
            state0 = jnp.zeros((b, DI, DS), delta.dtype)
            _, ys = jax.lax.scan(step, state0, xs)
            y = jnp.moveaxis(ys, 0, -1)
            y = y + D[None, :, None] * u
            y = y * jax.nn.silu(z)
            return jnp.swapaxes(y, 1, 2)
        key = jax.random.key(seed)
        ks = jax.random.split(key, 8)
        hidden_states = jax.random.normal(ks[0], (B, L, DM), jnp.float32)
        z = jax.random.normal(ks[1], (B, DI, L), jnp.float32)
        in_proj_w = jax.random.normal(ks[2], (DI, DM), jnp.float32) * DM ** (-0.5)
        conv_w = jax.random.normal(ks[3], (DI, DC), jnp.float32) * DC ** (-0.5)
        conv_b = jnp.zeros((DI,), jnp.float32)
        x_proj_w = jax.random.normal(ks[4], (DR + 2 * DS, DI), jnp.float32) * DI ** (-0.5)
        dt_std = DR ** (-0.5)
        dt_proj_w = jax.random.uniform(ks[5], (DI, DR), jnp.float32, -dt_std, dt_std)
        dt = jnp.exp(jax.random.uniform(ks[6], (DI,), jnp.float32) * (math.log(DT_MAX) - math.log(DT_MIN)) + math.log(DT_MIN))
        dt = jnp.clip(dt, DT_FLOOR)
        dt_proj_b = dt + jnp.log(-jnp.expm1(-dt))
        A_log = jnp.log(jnp.broadcast_to(jnp.arange(1, DS + 1, dtype=jnp.float32), (DI, DS)))
        D = jnp.ones((DI,), jnp.float32)
        return dict(hidden_states=hidden_states, z=z, in_proj_w=in_proj_w, conv_w=conv_w, conv_b=conv_b, x_proj_w=x_proj_w, dt_proj_w=dt_proj_w, dt_proj_b=dt_proj_b, A_log=A_log, D=D)
    _L0_xattn_all = _L0_xattn_setup()
    _L0_xattn_in = {k: v for k, v in _L0_xattn_all.items() if k in ('in_proj_w', 'conv_w', 'conv_b', 'x_proj_w', 'dt_proj_w', 'dt_proj_b', 'A_log', 'D')}
    del _L0_xattn_all

    def _L0_ffn_setup():
        import jax, jax.numpy as jnp
        import numpy as np
        N, S, D = (8, 256, 256)
        O = 256
        E = 8
        K = 2
        key = jax.random.key(seed)
        ks = jax.random.split(key, 5)
        scale_in = 1.0 / np.sqrt(D)
        x = jax.random.normal(ks[0], (N, S, D), dtype=jnp.float32)
        gate_w = jax.random.uniform(ks[1], (D, E), dtype=jnp.float32, minval=-scale_in, maxval=scale_in)
        gate_b = jax.random.uniform(ks[2], (E,), dtype=jnp.float32, minval=-scale_in, maxval=scale_in)
        expert_w = jax.random.uniform(ks[3], (E, D, O), dtype=jnp.float32, minval=-scale_in, maxval=scale_in)
        expert_b = jax.random.uniform(ks[4], (E, O), dtype=jnp.float32, minval=-scale_in, maxval=scale_in)
        return {'x': x, 'gate_w': gate_w, 'gate_b': gate_b, 'expert_w': expert_w, 'expert_b': expert_b}
    _L0_ffn_all = _L0_ffn_setup()
    _L0_ffn_in = {k: v for k, v in _L0_ffn_all.items() if k in ('gate_w', 'gate_b', 'expert_w', 'expert_b')}
    del _L0_ffn_all
    return {'x': x, 'ctx_1024': ctx_1024, 'g_xattn': g_xattn, 'g_ffn': g_ffn, 'L0_xattn_in_proj_w': _L0_xattn_in['in_proj_w'], 'L0_xattn_conv_w': _L0_xattn_in['conv_w'], 'L0_xattn_conv_b': _L0_xattn_in['conv_b'], 'L0_xattn_x_proj_w': _L0_xattn_in['x_proj_w'], 'L0_xattn_dt_proj_w': _L0_xattn_in['dt_proj_w'], 'L0_xattn_dt_proj_b': _L0_xattn_in['dt_proj_b'], 'L0_xattn_A_log': _L0_xattn_in['A_log'], 'L0_xattn_D': _L0_xattn_in['D'], 'L0_ffn_gate_w': _L0_ffn_in['gate_w'], 'L0_ffn_gate_b': _L0_ffn_in['gate_b'], 'L0_ffn_expert_w': _L0_ffn_in['expert_w'], 'L0_ffn_expert_b': _L0_ffn_in['expert_b']}

def reference(x, ctx_1024, g_xattn, g_ffn, L0_xattn_in_proj_w, L0_xattn_conv_w, L0_xattn_conv_b, L0_xattn_x_proj_w, L0_xattn_dt_proj_w, L0_xattn_dt_proj_b, L0_xattn_A_log, L0_xattn_D, L0_ffn_gate_w, L0_ffn_gate_b, L0_ffn_expert_w, L0_ffn_expert_b):
    import jax
    import jax.numpy as jnp

    def _L0_xattn_ref(hidden_states, z, in_proj_w, conv_w, conv_b, x_proj_w, dt_proj_w, dt_proj_b, A_log, D):
        import jax, jax.numpy as jnp
        import numpy as np
        import math
        B, L, DM = (2, 256, 128)
        DS, DC, EXP = (16, 4, 2)
        DI = EXP * DM
        DR = math.ceil(DM / 16)
        DT_MIN, DT_MAX, DT_FLOOR = (0.001, 0.1, 0.0001)

        def _ssm_forward(hidden_states, z, in_proj_w, conv_w, conv_b, x_proj_w, dt_proj_w, dt_proj_b, A_log, D):
            b = hidden_states.shape[0]
            x = jnp.einsum('ed,bld->bel', in_proj_w, hidden_states)
            xp = jnp.pad(x, ((0, 0), (0, 0), (DC - 1, 0)))
            xc = jax.lax.conv_general_dilated(xp, conv_w[:, None, :], window_strides=(1,), padding='VALID', dimension_numbers=('NCH', 'OIH', 'NCH'), feature_group_count=DI)
            u = jax.nn.silu(xc + conv_b[None, :, None])
            x_dbl = jnp.einsum('ke,bel->bkl', x_proj_w, u)
            dt_lo = x_dbl[:, :DR]
            Bm = x_dbl[:, DR:DR + DS]
            Cm = x_dbl[:, DR + DS:]
            delta = jax.nn.softplus(jnp.einsum('er,brl->bel', dt_proj_w, dt_lo) + dt_proj_b[None, :, None])
            A = -jnp.exp(A_log)

            def step(state, xs):
                d_t, B_t, C_t, u_t = xs
                dA = jnp.exp(d_t[..., None] * A)
                state = state * dA + (d_t * u_t)[..., None] * B_t[:, None, :]
                y_t = jnp.einsum('ben,bn->be', state, C_t)
                return (state, y_t)
            xs = (jnp.moveaxis(delta, -1, 0), jnp.moveaxis(Bm, -1, 0), jnp.moveaxis(Cm, -1, 0), jnp.moveaxis(u, -1, 0))
            state0 = jnp.zeros((b, DI, DS), delta.dtype)
            _, ys = jax.lax.scan(step, state0, xs)
            y = jnp.moveaxis(ys, 0, -1)
            y = y + D[None, :, None] * u
            y = y * jax.nn.silu(z)
            return jnp.swapaxes(y, 1, 2)
        return _ssm_forward(hidden_states, z, in_proj_w, conv_w, conv_b, x_proj_w, dt_proj_w, dt_proj_b, A_log, D)

    def _L0_ffn_ref(x, gate_w, gate_b, expert_w, expert_b):
        import jax, jax.numpy as jnp
        import numpy as np
        N, S, D = (8, 256, 256)
        O = 256
        E = 8
        K = 2
        gate_logits = jnp.einsum('nsd,de->nse', x, gate_w) + gate_b
        _, top_idx = jax.lax.top_k(gate_logits, K)
        all_out = jax.nn.relu(jnp.einsum('nsd,edo->nseo', x, expert_w) + expert_b)
        sel = jnp.take_along_axis(all_out, top_idx[..., None], axis=2)
        return sel.mean(axis=2)
    x = x + jnp.tanh(g_xattn[0]) * _L0_xattn_ref(ctx_1024, _layernorm(x, axis=-1), L0_xattn_in_proj_w, L0_xattn_conv_w, L0_xattn_conv_b, L0_xattn_x_proj_w, L0_xattn_dt_proj_w, L0_xattn_dt_proj_b, L0_xattn_A_log, L0_xattn_D)
    x = x + jnp.tanh(g_ffn[0]) * _L0_ffn_ref(_layernorm(x, axis=-1), L0_ffn_gate_w, L0_ffn_gate_b, L0_ffn_expert_w, L0_ffn_expert_b)
    return x

_drawn_inputs = setup_inputs


def setup_inputs(seed=0):
    import zlib

    import numpy as np

    out = dict(_drawn_inputs(seed))
    spreads = {'L0_xattn_conv_b': (0.0, 0.1), 'L0_xattn_D': (1.0, 0.2)}
    factors = {'L0_xattn_dt_proj_w': 3.029, 'L0_ffn_expert_b': 3.653}
    for name, (base, spread) in spreads.items():
        noise = np.random.default_rng([zlib.crc32(name.encode()), seed]).standard_normal(out[name].shape)
        drawn = base * np.exp(spread * noise) if base else spread * noise
        out[name] = jnp.asarray(drawn.astype(out[name].dtype))
    for name, factor in factors.items():
        out[name] = (out[name] * factor).astype(out[name].dtype)
    return out
```

```python
from contextlib import ExitStack

import concourse.bass as bass
from concourse import mybir

F32 = mybir.dt.float32
BF16 = mybir.dt.bfloat16
U32 = mybir.dt.uint32
ALU = mybir.AluOpType
ACT = mybir.ActivationFunctionType

P = 128
NB = 4
L = 256
DC = 4
DI = 256
DM = 128
NS = 16
DR = 8
NE = 8
H = DI // P
SPANS = 2
BS = NB // SPANS
W = BS * L
TS = W // P
XD = DR + 2 * NS
PARTS = 3
EPS = 1e-5
RESET = 1.0e30
A_LEAST = 1e-27

COLS = {}
_at = 0
for _name, _n in (("conv_w", H * DC), ("conv_b", H), ("dt_b", H), ("a_log", H * NS), ("d", H), ("g", 2),
                  ("gate_b", NE), ("gate_w", 2 * NE), ("iota", NE), ("power", TS * 2)):
    COLS[_name] = slice(_at, _at + _n)
    _at += _n
NCOLS = _at


def flamingo_block(nc, ctxt, inpt, xpt, dtwt, vecs, ident_in, pick_in, x_in, ew_in, eb_in, out):
    es = ExitStack()
    with es:
        def sb(name, shape, dt=F32):
            return es.enter_context(nc.sbuf_tensor(name, shape, dt))

        def sem(name):
            return es.enter_context(nc.semaphore(name))

        ctx = sb("ctx", [P, SPANS, W])
        w_in = sb("w_in", [P, DI])
        w_xp = sb("w_xp", [P, H, XD])
        w_dt = sb("w_dt", [DR, DI])
        vec = sb("vec", [P, NCOLS])
        ident = sb("ident", [P, P])
        pick = sb("pick", [PARTS * 32, 32], BF16)
        xs = sb("xs", [P, NB * 2, L])
        ew = sb("ew", [P, 2, NE * DI])
        eb = sb("eb", [P, NE * DI // P])
        spread = sb("spread", [PARTS * 32, 32, P], BF16)
        a_neg = sb("a_neg", [P, H * NS])
        a_exp = sb("a_exp", [P, H * NS])
        tanh_g = sb("tanh_g", [P, 2])
        half_tanh = sb("half_tanh", [P, 1])
        gate_z = sb("gate_z", [P, NB, 2, L])
        stats = sb("stats", [P, NB * 2, 6])
        moments = sb("moments", [P, NB * 2, 2])
        rstd = sb("rstd", [P, NB * 2])
        var_eps = sb("var_eps", [P, NB * 2])
        neg_mean_rstd = sb("neg_mean_rstd", [P, NB * 2])
        ebp = sb("ebp", [P, PARTS, NE * DI // P], BF16)
        eb_rest = sb("eb_rest", [P, NE * DI // P])
        eb_rows = sb("eb_rows", [PARTS, NE * DI], BF16)
        ones = sb("ones", [PARTS, P], BF16)
        conv = sb("conv", [P, SPANS, H, W])
        u = sb("u", [P, SPANS, H, W])
        dt_lo = sb("dt_lo", [DR, SPANS, W])
        bc_parts = sb("bc_parts", [PARTS * 32, SPANS, W], BF16)
        bc_rest = sb("bc_rest", [32, W])
        bc_mid = sb("bc_mid", [32, W], BF16)
        sp_abs = sb("sp_abs", [P, H, W])
        sp_relu = sb("sp_relu", [P, H, W])
        sp_exp = sb("sp_exp", [P, H, W])
        sp_ln = sb("sp_ln", [P, H, W])
        sp_rest = sb("sp_rest", [P, H, W])
        delta = sb("delta", [P, SPANS, H, W])
        du = sb("du", [P, SPANS, H, W])
        dbu = sb("dbu", [P, 2, H, W])
        state = sb("state", [P, 2, H, W])
        c_rows = sb("c_rows", [P, 2, W])
        sc_out = sb("sc_out", [P, 3, H, W])
        yz = sb("yz", [P, H, W])
        x1 = sb("x1", [P, NB * 2, L])
        stats2 = sb("stats2", [P, NB * 2, 6])
        moments2 = sb("moments2", [P, NB * 2, 2])
        var_eps2 = sb("var_eps2", [P, NB * 2])
        rstd2 = sb("rstd2", [P, NB * 2])
        xn = sb("xn", [P, NB * 2, L])
        xnt = sb("xnt", [P, NB * 2, 2, P])
        logits = sb("logits", [P, NB * 2, NE])
        top = sb("top", [P, NB * 2, 8])
        top_at = sb("top_at", [P, NB * 2, 8], U32)
        top_f = sb("top_f", [P, NB * 2, 8])
        mask0 = sb("mask0", [P, NB * 2, NE])
        mask1 = sb("mask1", [P, NB * 2, NE])
        mask = sb("mask", [P, NB * 2, NE])
        relus = sb("relus", [P, 2, 4, 2 * DI])
        res = sb("res", [P, NB * 2, L])

        banks = [es.enter_context(nc.psum_tensor(f"bank{i}", [P, 512], F32)) for i in range(8)]
        da = banks[0:2]
        ysum = banks[2:4]
        b_bank, c_bank = banks[4], banks[5]
        work = banks[6:8]

        ld_ctx = [sem(f"ld_ctx{q}") for q in range(SPANS)]
        ld_w = sem("ld_w")
        ld_vec = sem("ld_vec")
        ld_pick = sem("ld_pick")
        ld_x = sem("ld_x")
        ld_eb = sem("ld_eb")
        ld_ew = sem("ld_ew")
        eb_moved = sem("eb_moved")
        stored = sem("stored")
        spread_made = sem("spread_made")
        ones_made = sem("ones_made")
        eb_split = sem("eb_split")
        z_vars = sem("z_vars")
        z_rstd = sem("z_rstd")
        z_bias = sem("z_bias")
        z_gated = sem("z_gated")
        tanh_done = sem("tanh_done")
        a_exped = sem("a_exped")
        a_made = sem("a_made")
        tap_done = sem("tap_done")
        conv_done = sem("conv_done")
        u_done = sem("u_done")
        dt_copied = sem("dt_copied")
        rest_made = sem("rest_made")
        parts_act = sem("parts_act")
        parts_made = sem("parts_made")
        sp_in = sem("sp_in")
        sp_exped = sem("sp_exped")
        sp_lned = sem("sp_lned")
        delta_done = sem("delta_done")
        work_ready = sem("work_ready")
        work_free = [sem(f"work_free{s}") for s in range(2)]
        b_ready, b_used = sem("b_ready"), sem("b_used")
        c_ready, c_copied = sem("c_ready"), sem("c_copied")
        da_ready = sem("da_ready")
        scanned = sem("scanned")
        scaled = sem("scaled")
        summed = sem("summed")
        y_read = sem("y_read")
        yz_done = sem("yz_done")
        x1_vars = sem("x1_vars")
        x1_rstd = sem("x1_rstd")
        xn_done = sem("xn_done")
        masks_done = sem("masks_done")
        relu_done = sem("relu_done")
        res_done = sem("res_done")
        dve_step = sem("dve_step")
        pool_step = sem("pool_step")
        act_step = sem("act_step")

        def v(name, i=None):
            s = vec[:, COLS[name]]
            return s if i is None else s[:, i:i + 1]

        items = []
        for q in range(SPANS):
            items += [("in", q, h) for h in range(H)]
        for q in range(SPANS):
            items += [("xd", q, 0)]
            items += [("dt", q, h) for h in range(H)]
        for q in range(SPANS):
            items += [("yt", q, b) for b in range(BS)]
            items += [("xt", q, b) for b in range(BS)]
            items += [("gate", q, 0)]
            items += [("moe", q, k) for k in range(TS * 4)]
        order = {item: k for k, item in enumerate(items)}

        def bank_of(*item):
            return work[order[item] % 2]

        def open_item(pe, *item):
            k = order[item]
            if k >= 2:
                pe.wait_ge(work_free[k % 2], k // 2)
            return work[k % 2]

        def await_item(eng, *item):
            eng.wait_ge(work_ready, order[item] + 1)
            return work[order[item] % 2]

        def await_read(eng, *item):
            k = order[item]
            eng.wait_ge(work_free[k % 2], k // 2 + 1)

        def free_of(*item):
            return work_free[order[item] % 2]

        FIRST = 7

        def moe_units(n):
            if n < FIRST:
                return range(0)
            per = TS * 4 / (NS - FIRST)
            return range(int(round((n - FIRST) * per)), int(round((n - FIRST + 1) * per)))

        block = es.enter_context(nc.Block())

        @block.sync
        def _(sp):
            sp.dma_start(w_in[:], inpt).then_inc(ld_w, 16)
            sp.dma_start(ctx[:, 0, :], ctxt[:, 0:W]).then_inc(ld_ctx[0], 16)
            sp.dma_start(ctx[:, 1, :], ctxt[:, W:2 * W]).then_inc(ld_ctx[1], 16)
            sp.dma_start(w_xp[:], xpt.rearrange("(h p) k -> p h k", p=P)).then_inc(ld_w, 16)
            sp.dma_start(w_dt[:], dtwt).then_inc(ld_w, 16)
            sp.dma_start(ident[:], ident_in).then_inc(ld_w, 16)
            sp.dma_start(ew[:], ew_in).then_inc(ld_ew, 16)
            sp.wait_ge(eb_split, 5)
            for part in range(PARTS):
                sp.dma_start(eb_rows[part:part + 1, :], ebp[:, part, :]).then_inc(eb_moved, 16)
            for t in range(NB * 2):
                sp.wait_ge(res_done, t + 1)
                sp.dma_start(out[t // 2, (t % 2) * P:(t % 2 + 1) * P, :], res[:, t, :]).then_inc(stored, 16)
            sp.wait_ge(stored, 16 * NB * 2)

        @block.gpsimd
        def _(pool):
            nc.gpsimd.memset(ones[:], 1.0).then_inc(ones_made, 1)
            pool.wait_ge(ld_pick, 16)
            nc.gpsimd.tensor_copy(spread[:], pick[:].rearrange("p (r a) -> p r a", a=1).broadcast_to(
                [PARTS * 32, 32, P])).then_inc(spread_made, 1)
            pool.wait_ge(ld_eb, 16)
            nc.gpsimd.tensor_copy(ebp[:, 0, :], eb[:]).then_inc(eb_split, 1)
            pool.wait_ge(eb_split, 1)
            nc.gpsimd.tensor_tensor(eb_rest[:], eb[:], ebp[:, 0, :], ALU.subtract).then_inc(eb_split, 1)
            pool.wait_ge(eb_split, 2)
            nc.gpsimd.tensor_copy(ebp[:, 1, :], eb_rest[:]).then_inc(eb_split, 1)
            pool.wait_ge(eb_split, 3)
            nc.gpsimd.tensor_tensor(eb[:], eb_rest[:], ebp[:, 1, :], ALU.subtract).then_inc(eb_split, 1)
            pool.wait_ge(eb_split, 4)
            nc.gpsimd.tensor_copy(ebp[:, 2, :], eb[:]).then_inc(eb_split, 1)
            pool.wait_ge(ld_vec, 16)
            pool.wait_ge(z_vars, 1)
            nc.gpsimd.tensor_tensor(rstd[:], var_eps[:], v("power"), ALU.pow).then_inc(z_rstd, 1)

            def power(q):
                tiles = slice(q * TS, (q + 1) * TS)
                pool.wait_ge(x1_vars, q + 1)
                nc.gpsimd.tensor_tensor(rstd2[:, tiles], var_eps2[:, tiles], v("power")[:, 0:TS],
                                        ALU.pow).then_inc(x1_rstd, 1)

            for i in range(SPANS * NS):
                pool.wait_ge(scanned, 2 * i + 2)
                pool.wait_ge(c_copied, i + 1)
                if i >= 3:
                    pool.wait_ge(summed, i - 2)
                c_wide = c_rows[:, i % 2, :].rearrange("p (a w) -> p a w", a=1).broadcast_to([P, H, W])
                nc.gpsimd.tensor_tensor(sc_out[:, i % 3], state[:, i % 2], c_wide, ALU.mult).then_inc(scaled, 1)
                if i == NS + 3:
                    power(0)
            power(1)

        @block.scalar
        def _(act):
            act.dma_start(vec[:], vecs).then_inc(ld_vec, 16)
            act.dma_start(pick[:], pick_in).then_inc(ld_pick, 16)
            act.dma_start(xs[:], x_in.rearrange("b (t p) l -> p (b t) l", p=P)).then_inc(ld_x, 16)
            act.dma_start(eb[:], eb_in.rearrange("e (a c) -> (e a) c", c=NE * DI // P)).then_inc(ld_eb, 16)

            act.wait_ge(ld_vec, 16)
            nc.scalar.activation(tanh_g[:], v("g"), ACT.Tanh).then_inc(tanh_done, 1)
            for q in range(SPANS):
                for h in range(H):
                    ps = await_item(act, "in", q, h)
                    nc.scalar.activation(conv[:, q, h, :], ps[:], ACT.Identity, bias=v("conv_b", h),
                                         scale=v("conv_w", h * DC + DC - 1)).then_inc(tap_done, 1)
                for h in range(H):
                    act.wait_ge(conv_done, 2 * q + h + 1)
                    nc.scalar.activation(u[:, q, h, :], conv[:, q, h, :], ACT.Silu).then_inc(u_done, 1)
            act.wait_ge(z_bias, 1)
            for t in range(NB * 2):
                nc.scalar.activation(gate_z[:, t // 2, t % 2, :], xs[:, t, :], ACT.Silu, scale=rstd[:, t:t + 1],
                                     bias=neg_mean_rstd[:, t:t + 1]).then_inc(z_gated, 1)
            nc.scalar.activation(a_exp[:], v("a_log"), ACT.Exp).then_inc(a_exped, 1)

            def softplus(q):
                act.wait_ge(rest_made, q + 1)
                nc.scalar.activation(bc_parts[32:64, q, :], bc_rest[:], ACT.Copy).then_inc(parts_act, 1)
                for h in range(H):
                    k = 2 * q + h
                    ps = await_item(act, "dt", q, h)
                    if q:
                        act.wait_ge(delta_done, q)
                    nc.scalar.activation(sp_abs[:, h, :], ps[:], ACT.Abs, bias=v("dt_b", h)).then_inc(act_step, 1)
                    nc.scalar.activation(sp_relu[:, h, :], ps[:], ACT.Relu, bias=v("dt_b", h)).then_inc(
                        free_of("dt", q, h), 1)
                    act.wait_ge(act_step, k + 1)
                    nc.scalar.activation(sp_exp[:, h, :], sp_abs[:, h, :], ACT.Exp, scale=-1.0).then_inc(sp_exped, 1)
                for h in range(H):
                    act.wait_ge(sp_exped, 2 * q + h + 1)
                    nc.scalar.activation(sp_ln[:, h, :], sp_exp[:, h, :], ACT.Ln, bias=1.0).then_inc(sp_lned, 1)

            def relu_unit(q, k):
                tile, pair = q * TS + k // 4, k % 4
                if pair == 0 and tile >= 2:
                    act.wait_ge(res_done, tile - 1)
                ps = await_item(act, "moe", q, k)
                act.wait_ge(masks_done, q + 1)
                for j in range(2):
                    e = 2 * pair + j
                    ins = nc.scalar.activation(relus[:, tile % 2, pair, j * DI:(j + 1) * DI],
                                               ps[:, j * DI:(j + 1) * DI], ACT.Relu, scale=mask[:, tile, e:e + 1])
                    if j == 0:
                        ins.then_inc(relu_done, 1)
                    else:
                        ins.then_inc(free_of("moe", q, k), 1)

            def copy_xnt(q):
                for b in range(BS):
                    ps = await_item(act, "xt", q, b)
                    t = q * TS + 2 * b
                    nc.scalar.activation(xnt[:, t:t + 2], ps[:].rearrange("p (t k c) -> p t k c", t=2, k=2),
                                         ACT.Copy).then_inc(free_of("xt", q, b), 1)

            softplus(0)
            softplus(1)
            for q in range(SPANS):
                for n in range(NS):
                    i = q * NS + n
                    if n == 0:
                        act.wait_ge(delta_done, q + 1)
                        act.wait_ge(a_made, 1)
                    for h in range(H):
                        if i >= 1:
                            act.wait_ge(scanned, 2 * (i - 1) + h + 1)
                        nc.scalar.activation(da[h][:], delta[:, q, h, :], ACT.Exp,
                                             scale=a_neg[:, h * NS + n:h * NS + n + 1]).then_inc(da_ready, 1)
                    act.wait_ge(c_ready, i + 1)
                    if i >= 2:
                        act.wait_ge(scaled, i - 1)
                    nc.scalar.activation(c_rows[:, i % 2, :], c_bank[:], ACT.Copy).then_inc(c_copied, 1)
                    if q == 1:
                        if n == 5:
                            copy_xnt(0)
                        for k in moe_units(n):
                            relu_unit(0, k)
            copy_xnt(1)
            for k in range(TS * 4):
                relu_unit(1, k)

        @block.vector
        def _(dve):
            steps = [0]

            def link(ins):
                steps[0] += 1
                ins.then_inc(dve_step, 1)
                dve.wait_ge(dve_step, steps[0])

            dve.wait_ge(ld_x, 16)
            for t in range(NB * 2):
                last = nc.vector.bn_stats(stats[:, t, :], xs[:, t, :])
            link(last)
            for t in range(NB * 2):
                last = nc.vector.bn_aggr(moments[:, t, :], stats[:, t, :])
            link(last)
            nc.vector.tensor_scalar(var_eps[:], moments[:, :, 1], EPS, None, ALU.add).then_inc(z_vars, 1)

            def convolve(q):
                for h in range(H):
                    dve.wait_ge(tap_done, 2 * q + h + 1)
                    ps = bank_of("in", q, h)[:].rearrange("p (b l) -> p b l", b=BS)
                    acc = conv[:, q, h, :].rearrange("p (b l) -> p b l", b=BS)
                    for lag in range(1, DC):
                        if lag < DC - 1:
                            link(nc.vector.scalar_tensor_tensor(
                                out=acc[:, :, lag:], in0=ps[:, :, :L - lag],
                                scalar=v("conv_w", h * DC + DC - 1 - lag), in1=acc[:, :, lag:], op0=ALU.mult,
                                op1=ALU.add))
                        else:
                            nc.vector.scalar_tensor_tensor(
                                out=acc[:, :, lag:], in0=ps[:, :, :L - lag],
                                scalar=v("conv_w", h * DC + DC - 1 - lag), in1=acc[:, :, lag:], op0=ALU.mult,
                                op1=ALU.add).then_inc(conv_done, 1)
                    dve.wait_ge(conv_done, 2 * q + h + 1)
                    dve.sem_inc(free_of("in", q, h), 1)

            convolve(0)
            convolve(1)
            dve.wait_ge(z_rstd, 1)
            nc.vector.scalar_tensor_tensor(out=neg_mean_rstd[:], in0=moments[:, :, 0], scalar=-1.0, in1=rstd[:],
                                           op0=ALU.mult, op1=ALU.mult).then_inc(z_bias, 1)
            dve.wait_ge(a_exped, 1)
            nc.vector.tensor_scalar(a_neg[:], a_exp[:], A_LEAST, -1.0, ALU.max, ALU.mult).then_inc(a_made, 1)

            def split_bc(q):
                ps = await_item(dve, "xd", q, 0)
                nc.vector.tensor_copy(dt_lo[:, q, :], ps[2 * NS:2 * NS + DR, :]).then_inc(dt_copied, 1)
                if q:
                    dve.wait_ge(parts_act, q)
                link(nc.vector.tensor_copy(bc_parts[0:32, q, :], ps[0:32, :]))
                nc.vector.tensor_tensor(bc_rest[:], ps[0:32, :], bc_parts[0:32, q, :], ALU.subtract).then_inc(
                    rest_made, 1)
                dve.wait_ge(rest_made, q + 1)
                link(nc.vector.tensor_copy(bc_mid[:], bc_rest[:]))
                nc.vector.tensor_tensor(bc_parts[64:96, q, :], bc_rest[:], bc_mid[:], ALU.subtract).then_inc(
                    parts_made, 1)
                dve.wait_ge(parts_made, q + 1)
                dve.sem_inc(free_of("xd", q, 0), 1)

            def finish_delta(q):
                for h in range(H):
                    dve.wait_ge(sp_exped, 2 * q + h + 1)
                    link(nc.vector.tensor_scalar(sp_rest[:, h, :], sp_exp[:, h, :], 1.0, -1.0, ALU.add, ALU.add))
                    link(nc.vector.tensor_tensor(sp_rest[:, h, :], sp_exp[:, h, :], sp_rest[:, h, :], ALU.subtract))
                for h in range(H):
                    dve.wait_ge(sp_lned, 2 * q + h + 1)
                    link(nc.vector.tensor_tensor(sp_rest[:, h, :], sp_ln[:, h, :], sp_rest[:, h, :], ALU.add))
                    link(nc.vector.tensor_tensor(delta[:, q, h, :], sp_relu[:, h, :], sp_rest[:, h, :], ALU.add))
                dve.wait_ge(u_done, 2 * q + 2)
                link(nc.vector.tensor_tensor(du[:, q], delta[:, q], u[:, q], ALU.mult))
                first = delta[:, q].rearrange("p h (b l) -> p h b l", b=BS)[:, :, :, 0]
                nc.vector.memset(first, RESET).then_inc(delta_done, 1)

            split_bc(0)
            split_bc(1)
            finish_delta(0)
            finish_delta(1)
            dve.wait_ge(tanh_done, 1)
            link(nc.vector.tensor_scalar(half_tanh[:], tanh_g[:, 1:2], 0.5, None, ALU.mult))

            def make_dbu(i):
                q = i // NS
                dve.wait_ge(b_ready, i + 1)
                if i >= 2:
                    dve.wait_ge(scanned, 2 * (i - 1))
                b_wide = b_bank[:].rearrange("p (a w) -> p a w", a=1).broadcast_to([P, H, W])
                nc.vector.tensor_tensor(dbu[:, i % 2], b_wide, du[:, q], ALU.mult).then_inc(b_used, 1)

            def scan(i):
                for h in range(H):
                    dve.wait_ge(b_used, i + 1)
                    dve.wait_ge(da_ready, 2 * i + h + 1)
                    if i >= 2:
                        dve.wait_ge(scaled, i - 1)
                    nc.vector.tensor_tensor_scan(state[:, i % 2, h, :], da[h][:], dbu[:, i % 2, h, :], 0.0,
                                                 ALU.mult, ALU.add).then_inc(scanned, 1)

            def gate_y(q):
                dve.wait_ge(summed, (q + 1) * NS)
                for h in range(H):
                    link(nc.vector.scalar_tensor_tensor(out=conv[:, q, h, :], in0=u[:, q, h, :], scalar=v("d", h),
                                                        in1=ysum[h][:], op0=ALU.mult, op1=ALU.add))
                dve.sem_inc(y_read, 1)
                dve.wait_ge(z_gated, NB * 2)
                for h in range(H):
                    nc.vector.tensor_tensor(yz[:, h, :].rearrange("p (b l) -> p b l", b=BS),
                                            conv[:, q, h, :].rearrange("p (b l) -> p b l", b=BS),
                                            gate_z[:, q * BS:(q + 1) * BS, h, :], ALU.mult).then_inc(yz_done, 1)

            def residual(q):
                for b in range(BS):
                    ps = await_item(dve, "yt", q, b)
                    t = q * TS + 2 * b
                    nc.vector.scalar_tensor_tensor(out=x1[:, t:t + 2, :], in0=ps[:].rearrange("p (t c) -> p t c", t=2),
                                                   scalar=tanh_g[:, 0:1], in1=xs[:, t:t + 2, :], op0=ALU.mult,
                                                   op1=ALU.add).then_inc(free_of("yt", q, b), 1)
                for b in range(BS):
                    await_read(dve, "yt", q, b)
                for t in range(q * TS, (q + 1) * TS):
                    last = nc.vector.bn_stats(stats2[:, t, :], x1[:, t, :])
                link(last)
                for t in range(q * TS, (q + 1) * TS):
                    last = nc.vector.bn_aggr(moments2[:, t, :], stats2[:, t, :])
                link(last)
                tiles = slice(q * TS, (q + 1) * TS)
                nc.vector.tensor_scalar(var_eps2[:, tiles], moments2[:, tiles, 1], EPS, None, ALU.add).then_inc(
                    x1_vars, 1)

            def normalize(q):
                dve.wait_ge(x1_rstd, q + 1)
                for t in range(q * TS, (q + 1) * TS):
                    nc.vector.tensor_scalar(xn[:, t, :], x1[:, t, :], moments2[:, t, 0:1], rstd2[:, t:t + 1],
                                            ALU.subtract, ALU.mult).then_inc(xn_done, 1)

            def choose(q):
                tiles = slice(q * TS, (q + 1) * TS)
                ps = await_item(dve, "gate", q, 0)
                gate_b = v("gate_b").rearrange("p (a e) -> p a e", a=1).broadcast_to([P, TS, NE])
                link(nc.vector.tensor_tensor(logits[:, tiles, :], ps[:, 0:TS * NE].rearrange("p (t e) -> p t e", t=TS),
                                             gate_b, ALU.add))
                dve.sem_inc(free_of("gate", q, 0), 1)
                for t in range(q * TS, (q + 1) * TS):
                    last = nc.vector.max(top[:, t, :], logits[:, t, :])
                link(last)
                for t in range(q * TS, (q + 1) * TS):
                    last = nc.vector.max_index(top_at[:, t, :], top[:, t, :], logits[:, t, :])
                link(last)
                link(nc.vector.tensor_copy(top_f[:, tiles, 0:2], top_at[:, tiles, 0:2]))
                iota = v("iota").rearrange("p (a e) -> p a e", a=1).broadcast_to([P, TS, NE])
                for m, place in ((mask0, 0), (mask1, 1)):
                    last = nc.vector.tensor_tensor(m[:, tiles, :], iota,
                                                   top_f[:, tiles, place:place + 1].broadcast_to([P, TS, NE]),
                                                   ALU.is_equal)
                link(last)
                nc.vector.tensor_tensor(mask[:, tiles, :], mask0[:, tiles, :], mask1[:, tiles, :],
                                        ALU.add).then_inc(masks_done, 1)

            def finish_tile(t):
                s = t % 2
                for pair in (2, 3):
                    await_read(dve, "moe", t // TS, (t % TS) * 4 + pair)
                dve.wait_ge(relu_done, 4 * t + 4)
                for a, b in ((0, 1), (2, 3)):
                    last = nc.vector.tensor_tensor(relus[:, s, a], relus[:, s, a], relus[:, s, b], ALU.add)
                link(last)
                link(nc.vector.tensor_tensor(relus[:, s, 0], relus[:, s, 0], relus[:, s, 2], ALU.add))
                nc.vector.tensor_tensor(relus[:, s, 1, 0:DI], relus[:, s, 0, 0:DI], relus[:, s, 0, DI:], ALU.add).then_inc(
                    dve_step, 1)
                steps[0] += 1
                dve.wait_ge(dve_step, steps[0])
                nc.vector.scalar_tensor_tensor(out=res[:, t, :], in0=relus[:, s, 1, 0:DI], scalar=half_tanh[:, 0:1],
                                               in1=x1[:, t, :], op0=ALU.mult, op1=ALU.add).then_inc(res_done, 1)

            make_dbu(0)
            for i in range(SPANS * NS):
                if i + 1 < SPANS * NS:
                    make_dbu(i + 1)
                scan(i)
                n = i - NS
                if n == 1:
                    gate_y(0)
                if n == 2:
                    residual(0)
                if n == 4:
                    normalize(0)
                if n == 6:
                    choose(0)
                if n >= 0:
                    for t in range(TS):
                        if 4 * t + 3 in moe_units(n - 1):
                            finish_tile(t)
            for t in range(TS):
                if 4 * t + 3 in moe_units(NS - 1):
                    finish_tile(t)
            gate_y(1)
            residual(1)
            normalize(1)
            choose(1)
            for t in range(TS, 2 * TS):
                finish_tile(t)

        @block.tensor
        def _(pe):
            pe.wait_ge(ld_w, 64)
            for q in range(SPANS):
                pe.wait_ge(ld_ctx[q], 16)
                for h in range(H):
                    ps = open_item(pe, "in", q, h)
                    nc.tensor.matmul(ps[:], w_in[:, h * P:(h + 1) * P], ctx[:, q, :], start=True,
                                     stop=True).then_inc(work_ready, 1)
            for q in range(SPANS):
                pe.wait_ge(u_done, 2 * q + 2)
                ps = open_item(pe, "xd", q, 0)
                for h in range(H):
                    ins = nc.tensor.matmul(ps[0:XD, :], w_xp[:, h, :], u[:, q, h, :], start=(h == 0),
                                           stop=(h == H - 1))
                ins.then_inc(work_ready, 1)
                pe.wait_ge(dt_copied, q + 1)
                for h in range(H):
                    ps = open_item(pe, "dt", q, h)
                    nc.tensor.matmul(ps[:], w_dt[:, h * P:(h + 1) * P], dt_lo[:, q, :], start=True,
                                     stop=True).then_inc(work_ready, 1)

            def spread_bc(i):
                q, n = i // NS, i % NS
                if i == 0:
                    pe.wait_ge(spread_made, 1)
                if n == 0:
                    pe.wait_ge(parts_made, q + 1)
                    pe.wait_ge(parts_act, q + 1)
                if i >= 1:
                    pe.wait_ge(b_used, i)
                nc.tensor.matmul(b_bank[:], spread[:, n, :], bc_parts[:, q, :], start=True, stop=True).then_inc(
                    b_ready, 1)
                if i >= 1:
                    pe.wait_ge(c_copied, i)
                nc.tensor.matmul(c_bank[:], spread[:, NS + n, :], bc_parts[:, q, :], start=True, stop=True).then_inc(
                    c_ready, 1)

            def sum_states(i):
                q, n = i // NS, i % NS
                pe.wait_ge(scaled, i + 1)
                if n == 0 and q:
                    pe.wait_ge(y_read, q)
                for h in range(H):
                    ins = nc.tensor.matmul(ysum[h][:], ident[:], sc_out[:, i % 3, h, :], start=(n == 0),
                                           stop=(n == NS - 1))
                ins.then_inc(summed, 1)

            def turn_y(q):
                pe.wait_ge(yz_done, 2 * q + 2)
                for b in range(BS):
                    ps = open_item(pe, "yt", q, b)
                    for t in range(2):
                        for h in range(H):
                            at = b * L + t * P
                            ins = nc.tensor.transpose(ps[:, (t * 2 + h) * P:(t * 2 + h + 1) * P],
                                                      yz[:, h, at:at + P], ident[:])
                    ins.then_inc(work_ready, 1)

            def turn_xn(q):
                for b in range(BS):
                    pe.wait_ge(xn_done, q * TS + 2 * b + 2)
                    ps = open_item(pe, "xt", q, b)
                    for t in range(2):
                        for k in range(2):
                            ins = nc.tensor.transpose(ps[:, (t * 2 + k) * P:(t * 2 + k + 1) * P],
                                                      xn[:, q * TS + 2 * b + t, k * P:(k + 1) * P], ident[:])
                    ins.then_inc(work_ready, 1)

            def gates(q):
                for b in range(BS):
                    await_read(pe, "xt", q, b)
                ps = open_item(pe, "gate", q, 0)
                gate_w = v("gate_w").rearrange("p (k e) -> p k e", k=2)
                for t in range(TS):
                    for k in range(2):
                        ins = nc.tensor.matmul(ps[:, t * NE:(t + 1) * NE], xnt[:, q * TS + t, k, :], gate_w[:, k, :],
                                               start=(k == 0), stop=(k == 1))
                ins.then_inc(work_ready, 1)

            def expert_pair(q, k):
                t, pair = q * TS + k // 4, k % 4
                cols = slice(pair * 2 * DI, (pair + 1) * 2 * DI)
                if k == 0 and q == 0:
                    pe.wait_ge(ld_ew, 16)
                    pe.wait_ge(eb_moved, 16 * PARTS)
                    pe.wait_ge(ones_made, 1)
                ps = open_item(pe, "moe", q, k)
                nc.tensor.matmul(ps[:], ones[:], eb_rows[:, cols], start=True, stop=False)
                for c in range(2):
                    ins = nc.tensor.matmul(ps[:], xnt[:, t, c, :], ew[:, c, cols], start=False, stop=(c == 1))
                ins.then_inc(work_ready, 1)

            spread_bc(0)
            for i in range(SPANS * NS):
                if i + 1 < SPANS * NS:
                    spread_bc(i + 1)
                if i >= 1:
                    sum_states(i - 1)
                n = i - NS
                if n == 2:
                    turn_y(0)
                if n == 5:
                    turn_xn(0)
                if n == 6:
                    gates(0)
                if n >= 0:
                    for k in moe_units(n):
                        expert_pair(0, k)
            sum_states(SPANS * NS - 1)
            turn_y(1)
            turn_xn(1)
            gates(1)
            for k in range(TS * 4):
                expert_pair(1, k)


def kernel(x, ctx_1024, g_xattn, g_ffn, L0_xattn_in_proj_w, L0_xattn_conv_w, L0_xattn_conv_b, L0_xattn_x_proj_w,
           L0_xattn_dt_proj_w, L0_xattn_dt_proj_b, L0_xattn_A_log, L0_xattn_D, L0_ffn_gate_w, L0_ffn_gate_b,
           L0_ffn_expert_w, L0_ffn_expert_b):
    import numpy as np
    import ml_dtypes
    import concourse.bacc as bacc
    from concourse.bass_utils import run_bass_kernel_spmd

    def halves(a):
        a = np.asarray(a).reshape(H, P, -1)
        return a.transpose(1, 0, 2).reshape(P, -1)

    def rows(a):
        return np.broadcast_to(np.asarray(a).reshape(1, -1), (P, np.asarray(a).size))

    vecs = np.concatenate([
        halves(L0_xattn_conv_w), halves(L0_xattn_conv_b), halves(L0_xattn_dt_proj_b), halves(L0_xattn_A_log),
        halves(L0_xattn_D), rows(g_xattn), rows(g_ffn), rows(L0_ffn_gate_b), halves(L0_ffn_gate_w),
        rows(np.arange(NE, dtype=np.float32)), rows(np.full(TS * 2, -0.5, np.float32))], axis=1)
    pick = np.tile(np.eye(32, dtype=ml_dtypes.bfloat16), (PARTS, 1))
    xp = np.asarray(L0_xattn_x_proj_w)
    arrays = {
        "ctxt": np.asarray(ctx_1024).transpose(2, 0, 1).reshape(DM, NB * L),
        "inpt": np.asarray(L0_xattn_in_proj_w).T,
        "xpt": np.concatenate([xp[DR:], xp[:DR]], axis=0).T,
        "dtwt": np.asarray(L0_xattn_dt_proj_w).T,
        "vecs": vecs,
        "ident_in": np.eye(P, dtype=np.float32),
        "pick_in": pick,
        "x_in": np.asarray(x),
        "ew_in": np.asarray(L0_ffn_expert_w).reshape(NE, 2, P, DI).transpose(2, 1, 0, 3).reshape(P, 2, NE * DI),
        "eb_in": np.asarray(L0_ffn_expert_b),
    }
    arrays = {k: np.ascontiguousarray(a) for k, a in arrays.items()}
    nc = bacc.Bacc("TRN2", target_bir_lowering=False, num_devices=1)
    aps = {k: nc.dram_tensor(k, a.shape, mybir.dt.from_np(a.dtype), kind="ExternalInput").ap()
           for k, a in arrays.items()}
    out = nc.dram_tensor("out", (NB, L, DI), F32, kind="ExternalOutput").ap()
    flamingo_block(nc, **aps, out=out)
    return run_bass_kernel_spmd(nc, [arrays], core_ids=[0]).results[0]["out"]
```

```python
from contextlib import ExitStack

import concourse.bass as bass
from concourse import mybir

F32 = mybir.dt.float32
BF16 = mybir.dt.bfloat16
U32 = mybir.dt.uint32
ALU = mybir.AluOpType
ACT = mybir.ActivationFunctionType

P = 128
NB = 4
L = 256
DC = 4
DI = 256
DM = 128
NS = 16
DR = 8
NE = 8
H = DI // P
STRIP = 32
NJ = P // STRIP
GC = P // NS
NK = STRIP // GC
SB = H * NK
STEPS = NB * SB
NT = L // P
XD = DR + 2 * P
BANK = 512
JB = BANK // L
NU = NJ // JB
PARTS = 3
EPS = 1e-5
RESET = 1.0e30
A_LEAST = 1e-27
PAIR = 2
UNITS = NT * NE
WORK = 3
PE_AHEAD = 2
ACT_AHEAD = 2
DA_RING = 4
RING = 4
DIRECT = 2
SUM_LAG = 3

COLS = {}
_at = 0
for _name, _n in (("conv_w", H * DC), ("conv_b", H), ("dt_b", H), ("a_log", H * NK * NJ), ("d", H), ("g", 2),
                  ("gate_b", NE), ("gate_w", 2 * NE), ("iota", NE), ("power", NB * H)):
    COLS[_name] = slice(_at, _at + _n)
    _at += _n
NCOLS = _at


FIRST = ("dt_lo", "b_rep", "dt0", "dt1", "c_rep")
PREPARE = (("dt_lo", -25), ("b_rep", -25), ("c_rep", -24), ("dt0", -24), ("dt1", -22), ("soft", -20), ("delta", -18),
           ("high", -17), ("rest", -17), ("mid", -13), ("low", -11))
PREPARE_1 = (("dt_lo", 1), ("b_rep", 1), ("c_rep", 1), ("dt0", 1), ("dt1", 1), ("soft", 1), ("delta", 3),
             ("high", 3), ("rest", 3), ("mid", 6), ("low", 6))
Z_AT = (("z_moments", 2), ("z_exp", 6), ("z", 10))
FINISH = (("gate", 4), ("yt", 5), ("residual", 7), ("normalize", 10), ("xt", 11), ("logits", 12), ("choose", 13))
UNITS_FROM = 12
UNITS_IN = 10
AHEAD = (("yt", 4), ("residual", 1), ("normalize", 4), ("xt", 0), ("logits", 2), ("choose", 0))


def extra(b, unit):
    tile, e = divmod(unit, NE)
    return {NE // 2 - 1: [("fold", b, tile)], NE - 1: [("combine", b, tile)]}.get(e, [])


def schedule():
    banks = NU * SB
    last = NB * banks
    at = [[] for _ in range(last + 1)]
    for b in range(NB):
        for name, bank in Z_AT:
            at[banks * b + bank].append((name, b))
    for b in range(1, NB):
        for name, bank in PREPARE_1 if b == 1 else PREPARE:
            at[(0 if b == 1 else banks * b) + bank].append((name, b))
    left = []
    for b in range(NB - 1):
        for name, bank in FINISH:
            at[banks * (b + 1) + bank].append((name, b))
        for unit in range(UNITS):
            here = [("expert", b, unit)] + extra(b, unit)
            bank = banks * (b + 1) + UNITS_FROM + unit * UNITS_IN // UNITS
            if bank < last:
                at[bank] += here
            else:
                left += here
    b = NB - 1
    tail = at[last]
    tail.append(("gate", b))
    for name, ahead in AHEAD:
        tail += left[:ahead] + [(name, b)]
        left = left[ahead:]
    tail += left
    for unit in range(UNITS):
        tail += [("expert", b, unit)] + extra(b, unit)
    return at


SCHEDULE = schedule()


def flamingo_block(nc, ctxt, inpt, xpt, dtwt, vecs, ident_in, pick_in, gather_in, direct_in, x_in, ew_in, eb_in, out):
    es = ExitStack()
    with es:
        def sb(name, shape, dt=F32):
            return es.enter_context(nc.sbuf_tensor(name, shape, dt))

        def pb(name, shape):
            return es.enter_context(nc.psum_tensor(name, shape, F32))

        def sem(name):
            return es.enter_context(nc.semaphore(name))

        turn = nc.dram_tensor("turn", (NB, PARTS * 2 * H, P, L), BF16).ap()

        ctx = sb("ctx", [P, NB * L])
        w_in = sb("w_in", [P, DI])
        w_xp = sb("w_xp", [P, H, XD])
        w_dt = sb("w_dt", [DR, DI])
        vec = sb("vec", [P, NCOLS])
        ident = sb("ident", [P, P])
        spread = sb("spread", [PARTS * STRIP, NK, P], BF16)
        gather = sb("gather", [P, NK, STRIP])
        direct = sb("direct", [P, DIRECT, NJ, P])
        xs = sb("xs", [P, NB, H, L])
        ew = sb("ew", [P, 2, NE * DI])
        eb = sb("eb", [P, NE * DI // P])
        a_exp = sb("a_exp", [P, H * NK * NJ])
        a_neg = sb("a_neg", [P, H * NK * NJ])
        tanh_g = sb("tanh_g", [P, 2])
        half_tanh = sb("half_tanh", [P, 1])
        gate_z = sb("gate_z", [P, 2, H, L])
        z_norm = sb("z_norm", [P, H, L])
        stats = sb("stats", [P, NB * H, 6])
        moments = sb("moments", [P, NB * H, 2])
        var_eps = sb("var_eps", [P, NB * H])
        rstd = sb("rstd", [P, NB * H])
        neg_mean = sb("neg_mean", [P, NB * H])
        neg_mean_rstd = sb("neg_mean_rstd", [P, NB * H])
        ebp = sb("ebp", [P, PARTS, NE * DI // P], BF16)
        eb_rest = sb("eb_rest", [P, NE * DI // P])
        eb_rows = sb("eb_rows", [PARTS, NE * DI], BF16)
        ones = sb("ones", [PARTS, P], BF16)
        conv = sb("conv", [P, H, NB * L])
        u = sb("u", [P, NB, H, L])
        dt_lo = sb("dt_lo", [DR, 2, L])
        b_rep = sb("b_rep", [P, 3, L])
        c_rep = sb("c_rep", [P, 3, L])
        sp_abs = sb("sp_abs", [P, H, L])
        sp_relu = sb("sp_relu", [P, H, L])
        sp_exp = sb("sp_exp", [P, H, L])
        sp_ln = sb("sp_ln", [P, H, L])
        sp_rest = sb("sp_rest", [P, H, L])
        sp_fix = sb("sp_fix", [P, H, L])
        vals = sb("vals", [P, 2, H, L])
        vals_rest = sb("vals_rest", [P, 2, H, L])
        parts = sb("parts", [P, 2, PARTS, 2, H, L], BF16)
        stack = sb("stack", [PARTS * STRIP, 2, 2, H * NJ, L], BF16)
        da = sb("da", [P, DA_RING, BANK])
        dbu = sb("dbu", [P, 3, BANK])
        state = sb("state", [P, RING, NJ * L])
        scaled_state = sb("scaled_state", [P, RING, NJ, L])
        yd = ctx[:, 0:H * L].rearrange("p (h l) -> p h l", h=H)
        yz = ctx[:, H * L:2 * H * L].rearrange("p (h l) -> p h l", h=H)
        x1 = sb("x1", [P, NB, NT, DI])
        stats2 = sb("stats2", [P, NB, NT, 6])
        moments2 = sb("moments2", [P, NB, NT, 2])
        var_eps2 = sb("var_eps2", [P, NB, NT])
        rstd2 = sb("rstd2", [P, NB, NT])
        xn = sb("xn", [P, NT, DI])
        xnt = sb("xnt", [P, NB, NT, 2, P])
        logits = sb("logits", [P, NT, NE])
        top = sb("top", [P, NT, 8])
        top_at = sb("top_at", [P, NT, 8], U32)
        top_f = sb("top_f", [P, NT, 2])
        mask0 = sb("mask0", [P, NT, NE])
        mask1 = sb("mask1", [P, NT, NE])
        mask = sb("mask", [P, NB, NT, NE])
        relus = sb("relus", [P, 2, NE * DI])

        delta_ps = pb("delta_ps", [P, 2, BANK])
        du_ps = pb("du_ps", [P, 2, BANK])
        y_ps = pb("y_ps", [P, H, L])
        work = pb("work", [P, WORK, BANK])

        ld_ctx = [sem(f"ld_ctx{q}") for q in range(NB // PAIR)]
        ld_w, ld_xp, ld_vec, ld_sel, ld_x = sem("ld_w"), sem("ld_xp"), sem("ld_vec"), sem("ld_sel"), sem("ld_x")
        ld_direct = sem("ld_direct")
        ld_eb, ld_ew, eb_moved = sem("ld_eb"), sem("ld_ew"), sem("eb_moved")
        turned_out = [sem(f"turned_out{part}") for part in range(PARTS)]
        turned_in, stored = sem("turned_in"), sem("stored")
        ones_made, eb_split = sem("ones_made"), sem("eb_split")
        z_vars, z_rstd, z_bias = sem("z_vars"), sem("z_rstd"), sem("z_bias")
        z_normed, z_exped, z_lned = sem("z_normed"), sem("z_exped"), sem("z_lned")
        z_sigmoid, z_gated = sem("z_sigmoid"), sem("z_gated")
        tanh_done, a_exped, a_made = sem("tanh_done"), sem("a_exped"), sem("a_made")
        in_ready, tap_done, conv_done = sem("in_ready"), sem("tap_done"), sem("conv_done")
        u_done = sem("u_done")
        sp_abs_done, sp_exped, sp_lned = sem("sp_abs_done"), sem("sp_exped"), sem("sp_lned")
        vals_done, high_done, rest_done, mid_done, low_done = (
            sem("vals_done"), sem("high_done"), sem("rest_done"), sem("mid_done"), sem("low_done"))
        work_ready = sem("work_ready")
        work_free = [sem(f"work_free{s}") for s in range(WORK)]
        delta_ready, du_ready, dbu_done, da_ready = (
            sem("delta_ready"), sem("du_ready"), sem("dbu_done"), sem("da_ready"))
        scanned, scaled, summed, y_read = sem("scanned"), sem("scaled"), sem("summed"), sem("y_read")
        yz_done, x1_vars, x1_rstd, xn_done = sem("yz_done"), sem("x1_vars"), sem("x1_rstd"), sem("xn_done")
        masks_done, folded, res_done = sem("masks_done"), sem("folded"), sem("res_done")
        dve_step = sem("dve_step")

        def in_bank(q, h):
            return (delta_ps[:, 0, :], delta_ps[:, 1, :], du_ps[:, 0, :], du_ps[:, 1, :])[q * H + h]

        def v(name, i=None):
            s = vec[:, COLS[name]]
            return s if i is None else s[:, i:i + 1]

        all_tasks = [(name, 0) for name in FIRST]
        all_tasks += [task for tasks in SCHEDULE for task in tasks]
        order = {}

        def enlist(*item):
            order[item] = len(order)

        for task in all_tasks:
            kind, b = task[0], task[1]
            if kind in ("dt_lo", "b_rep", "c_rep", "dt0", "dt1"):
                enlist(kind, b)
            elif kind == "yt":
                for t in range(NT):
                    enlist("yt", b, t)
            elif kind == "xt":
                for t in range(NT):
                    enlist("xt", b, t)
            elif kind == "logits":
                enlist("logits", b)
            elif kind == "expert":
                enlist(*task)

        def open_slot(pe, *item):
            k = order[item]
            if k >= WORK:
                pe.wait_ge(work_free[k % WORK], k // WORK)
            return work[:, k % WORK, 0:L]

        def await_slot(eng, *item):
            eng.wait_ge(work_ready, order[item] + 1)
            return work[:, order[item] % WORK, 0:L]

        def await_read(eng, *item):
            k = order[item]
            eng.wait_ge(work_free[k % WORK], k // WORK + 1)

        def free_of(*item):
            return work_free[order[item] % WORK]

        def fold(eng, alu, b, t):
            s = (b * NT + t) % 2
            for e in (NE // 2 - 2, NE // 2 - 1):
                await_read(eng, "expert", b, t * NE + e)
            alu.tensor_tensor(relus[:, s, 0:2 * DI], relus[:, s, 0:2 * DI], relus[:, s, 2 * DI:4 * DI],
                              ALU.add).then_inc(folded, 1)

        block = es.enter_context(nc.Block())

        @block.sync
        def _(sp):
            sp.dma_start(w_in[:], inpt).then_inc(ld_w, 16)
            for q in range(NB // PAIR):
                cols = slice(q * PAIR * L, (q + 1) * PAIR * L)
                sp.dma_start(ctx[:, cols], ctxt[:, cols]).then_inc(ld_ctx[q], 16)
            sp.dma_start(w_xp[:], xpt).then_inc(ld_xp, 16)
            sp.dma_start(w_dt[:], dtwt).then_inc(ld_xp, 16)
            sp.dma_start(spread[:], pick_in).then_inc(ld_sel, 16)
            sp.dma_start(gather[:], gather_in).then_inc(ld_sel, 16)
            sp.dma_start(direct[:], direct_in).then_inc(ld_direct, 16)
            sp.dma_start(ident[:], ident_in).then_inc(ld_sel, 16)

            def turn_parts(b):
                if b >= 2:
                    sp.wait_ge(delta_ready, NU * SB * (b - 1))
                    sp.wait_ge(du_ready, NU * SB * (b - 1))
                for part, done in enumerate((high_done, mid_done, low_done)):
                    sp.wait_ge(done, b + 1)
                    sp.dma_start(turn[b, part * 2 * H:(part + 1) * 2 * H].rearrange("a p l -> p a l"),
                                 parts[:, b % 2, part].rearrange("p v h l -> p (v h) l")).then_inc(turned_out[part], 16)
                    sp.wait_ge(turned_out[part], 16 * (b + 1))
                    source = turn[b, part * 2 * H:(part + 1) * 2 * H].rearrange("vh (j c) l -> c (vh j) l", c=STRIP)
                    sp.dma_start(stack[part * STRIP:(part + 1) * STRIP, b % 2].rearrange("c v n l -> c (v n) l"),
                                 source).then_inc(turned_in, 16)

            def store(b, t):
                sp.wait_ge(res_done, b * NT + t + 1)
                sp.dma_start(out[b, t * P:(t + 1) * P, :], x1[:, b, t, :]).then_inc(stored, 16)

            turn_parts(0)
            sp.dma_start(ew[:], ew_in).then_inc(ld_ew, 16)
            sp.wait_ge(eb_split, 5)
            for part in range(PARTS):
                sp.dma_start(eb_rows[part:part + 1, :], ebp[:, part, :]).then_inc(eb_moved, 16)
            for tasks in SCHEDULE:
                for task in tasks:
                    if task[0] == "low":
                        turn_parts(task[1])
                    if task[0] == "combine":
                        store(task[1], task[2])
            sp.wait_ge(turned_in, 16 * NB * PARTS)
            sp.wait_ge(stored, 16 * NB * NT)

        @block.gpsimd
        def _(pool):
            nc.gpsimd.memset(ones[:], 1.0).then_inc(ones_made, 1)
            pool.wait_ge(ld_eb, 16)
            nc.gpsimd.tensor_copy(ebp[:, 0, :], eb[:]).then_inc(eb_split, 1)
            pool.wait_ge(eb_split, 1)
            nc.gpsimd.tensor_tensor(eb_rest[:], eb[:], ebp[:, 0, :], ALU.subtract).then_inc(eb_split, 1)
            pool.wait_ge(eb_split, 2)
            nc.gpsimd.tensor_copy(ebp[:, 1, :], eb_rest[:]).then_inc(eb_split, 1)
            pool.wait_ge(eb_split, 3)
            nc.gpsimd.tensor_tensor(eb[:], eb_rest[:], ebp[:, 1, :], ALU.subtract).then_inc(eb_split, 1)
            pool.wait_ge(eb_split, 4)
            nc.gpsimd.tensor_copy(ebp[:, 2, :], eb[:]).then_inc(eb_split, 1)
            pool.wait_ge(ld_vec, 16)

            def rest(b):
                pool.wait_ge(high_done, b + 1)
                if b:
                    pool.wait_ge(mid_done, b)
                nc.gpsimd.tensor_tensor(vals_rest[:], vals[:], parts[:, b % 2, 0], ALU.subtract).then_inc(rest_done, 1)

            def low(b):
                pool.wait_ge(mid_done, b + 1)
                if b >= 2:
                    pool.wait_ge(turned_out[2], 16 * (b - 1))
                nc.gpsimd.tensor_tensor(parts[:, b % 2, 2], vals_rest[:], parts[:, b % 2, 1], ALU.subtract).then_inc(low_done, 1)

            def z_moments(b):
                pool.wait_ge(z_vars, b + 1)
                cols = slice(b * H, (b + 1) * H)
                nc.gpsimd.tensor_tensor(rstd[:, cols], var_eps[:, cols], v("power")[:, 0:H], ALU.pow).then_inc(z_rstd, 1)
                pool.wait_ge(z_rstd, b + 1)
                nc.gpsimd.tensor_tensor(neg_mean_rstd[:, cols], neg_mean[:, cols], rstd[:, cols],
                                        ALU.mult).then_inc(z_bias, 1)

            def power(b):
                pool.wait_ge(x1_vars, b + 1)
                nc.gpsimd.tensor_tensor(rstd2[:, b, :], var_eps2[:, b, :], v("power")[:, 0:NT],
                                        ALU.pow).then_inc(x1_rstd, 1)

            def fold_here(b, t):
                if b < NB - 1:
                    fold(pool, nc.gpsimd, b, t)

            run = {"z_moments": z_moments, "rest": rest, "low": low, "residual": power, "fold": fold_here}
            rest(0)
            low(0)
            for i in range(STEPS):
                b = i // SB
                pool.wait_ge(scanned, NU * (i + 1))
                if i >= RING:
                    pool.wait_ge(summed, i - RING + 1)
                c_wide = c_rep[:, b % 3, :].rearrange("p (a l) -> p a l", a=1).broadcast_to([P, NJ, L])
                nc.gpsimd.tensor_tensor(scaled_state[:, i % RING], state[:, i % RING, :].rearrange("p (j l) -> p j l", j=NJ),
                                        c_wide, ALU.mult).then_inc(scaled, 1)
                for task in SCHEDULE[NU * i] + SCHEDULE[NU * i + 1]:
                    if task[0] in run:
                        run[task[0]](*task[1:])
            for task in SCHEDULE[NU * STEPS]:
                if task[0] in run:
                    run[task[0]](*task[1:])

        @block.scalar
        def _(act):
            act.dma_start(vec[:], vecs).then_inc(ld_vec, 16)
            act.dma_start(xs[:], x_in.rearrange("b (h p) l -> p (b h) l", p=P)).then_inc(ld_x, 16)
            act.dma_start(eb[:], eb_in).then_inc(ld_eb, 16)

            nc.scalar.preload_act_table_set("silu_and_others")
            act.wait_ge(ld_vec, 16)
            nc.scalar.activation(tanh_g[:], v("g"), ACT.Tanh).then_inc(tanh_done, 1)

            for q in range(NB // PAIR):
                for h in range(H):
                    act.wait_ge(in_ready, H * q + h + 1)
                    nc.scalar.activation(conv[:, h, q * PAIR * L:(q + 1) * PAIR * L], in_bank(q, h), ACT.Identity,
                                         bias=v("conv_b", h), scale=v("conv_w", h * DC + DC - 1)).then_inc(tap_done, 1)

            def exp_delta(m):
                act.wait_ge(delta_ready, m + 1)
                if m >= DA_RING:
                    act.wait_ge(scanned, m - DA_RING + 1)
                for j in range(JB):
                    at = m % (NU * SB) * JB + j
                    cols = slice(j * L, (j + 1) * L)
                    ins = nc.scalar.activation(da[:, m % DA_RING, cols], delta_ps[:, m % 2, cols], ACT.Exp,
                                               scale=a_neg[:, at:at + 1])
                ins.then_inc(da_ready, 1)

            def activate_u(b):
                act.wait_ge(conv_done, H * (b // PAIR + 1))
                nc.scalar.activation(u[:, b], conv[:, :, b * L:(b + 1) * L], ACT.Silu).then_inc(u_done, 1)

            def exp_z(b):
                act.wait_ge(z_bias, b + 1)
                if b:
                    act.wait_ge(z_gated, b)
                if b >= 2:
                    act.wait_ge(yz_done, b - 1)
                for h in range(H):
                    t = b * H + h
                    ins = nc.scalar.activation(z_norm[:, h, :], xs[:, b, h, :], ACT.Identity, scale=rstd[:, t:t + 1],
                                               bias=neg_mean_rstd[:, t:t + 1])
                ins.then_inc(z_normed, 1)
                act.wait_ge(z_normed, b + 1)
                nc.scalar.activation(gate_z[:, b % 2], z_norm[:], ACT.Exp, scale=-1.0).then_inc(z_exped, 1)
                act.wait_ge(z_exped, b + 1)
                nc.scalar.activation(gate_z[:, b % 2], gate_z[:, b % 2], ACT.Ln, bias=1.0).then_inc(z_lned, 1)
                act.wait_ge(z_lned, b + 1)
                nc.scalar.activation(gate_z[:, b % 2], gate_z[:, b % 2], ACT.Exp, scale=-1.0).then_inc(z_sigmoid, 1)

            def copy_dt_lo(b):
                ps = await_slot(act, "dt_lo", b)
                nc.scalar.activation(dt_lo[:, b % 2, :], ps[0:DR, :], ACT.Copy).then_inc(free_of("dt_lo", b), 1)

            def copy_rep(name, rep, b):
                if b >= 3:
                    act.wait_ge(dbu_done, NU * SB * (b - 2))
                    act.wait_ge(scaled, SB * (b - 2))
                ps = await_slot(act, name, b)
                nc.scalar.activation(rep[:, b % 3, :], ps, ACT.Copy).then_inc(free_of(name, b), 1)

            def soften(h, b):
                ps = await_slot(act, f"dt{h}", b)
                if b:
                    act.wait_ge(vals_done, b)
                nc.scalar.activation(sp_abs[:, h, :], ps, ACT.Abs, bias=v("dt_b", h)).then_inc(sp_abs_done, 1)
                nc.scalar.activation(sp_relu[:, h, :], ps, ACT.Relu, bias=v("dt_b", h)).then_inc(
                    free_of(f"dt{h}", b), 1)

            def soft(b):
                act.wait_ge(sp_abs_done, H * (b + 1))
                nc.scalar.activation(sp_exp[:], sp_abs[:], ACT.Exp, scale=-1.0).then_inc(sp_exped, 1)
                act.wait_ge(sp_exped, b + 1)
                nc.scalar.activation(sp_ln[:], sp_exp[:], ACT.Ln, bias=1.0).then_inc(sp_lned, 1)

            def high(b):
                act.wait_ge(vals_done, b + 1)
                if b >= 2:
                    act.wait_ge(turned_out[0], 16 * (b - 1))
                nc.scalar.activation(parts[:, b % 2, 0], vals[:], ACT.Copy).then_inc(high_done, 1)

            def mid(b):
                act.wait_ge(rest_done, b + 1)
                if b >= 2:
                    act.wait_ge(turned_out[1], 16 * (b - 1))
                nc.scalar.activation(parts[:, b % 2, 1], vals_rest[:], ACT.Copy).then_inc(mid_done, 1)

            def copy_xnt(b):
                for t in range(NT):
                    ps = await_slot(act, "xt", b, t)
                    nc.scalar.activation(xnt[:, b, t], ps.rearrange("p (k c) -> p k c", k=2), ACT.Copy).then_inc(
                        free_of("xt", b, t), 1)

            def expert(b, unit):
                tile, e = b * NT + unit // NE, unit % NE
                if e == 0:
                    act.wait_ge(masks_done, b + 1)
                    if tile >= 2:
                        act.wait_ge(res_done, tile - 1)
                ps = await_slot(act, "expert", b, unit)
                nc.scalar.activation(relus[:, tile % 2, e * DI:(e + 1) * DI], ps, ACT.Relu,
                                     scale=mask[:, b, unit // NE, e:e + 1]).then_inc(free_of("expert", b, unit), 1)

            run = {"z_exp": exp_z, "dt_lo": copy_dt_lo, "b_rep": lambda b: copy_rep("b_rep", b_rep, b), "c_rep": lambda b: copy_rep("c_rep", c_rep, b),
                   "dt0": lambda b: soften(0, b), "dt1": lambda b: soften(1, b), "soft": soft, "high": high,
                   "mid": mid, "xt": copy_xnt, "expert": expert}
            activate_u(0)
            activate_u(1)
            run["dt_lo"](0)
            run["b_rep"](0)
            activate_u(2)
            activate_u(3)
            nc.scalar.preload_act_table_set("natural_log_exp_and_others")
            nc.scalar.activation(a_exp[:], v("a_log"), ACT.Exp).then_inc(a_exped, 1)
            for name in ("dt0", "dt1", "soft", "c_rep", "high", "mid"):
                run[name](0)
            act.wait_ge(a_made, 1)
            for m in range(ACT_AHEAD):
                exp_delta(m)
            for i in range(STEPS):
                for n in range(NU):
                    if NU * i + n + ACT_AHEAD < NU * STEPS:
                        exp_delta(NU * i + n + ACT_AHEAD)
                    for task in SCHEDULE[NU * i + n]:
                        if task[0] in run:
                            run[task[0]](*task[1:])
            for task in SCHEDULE[NU * STEPS]:
                if task[0] in run:
                    run[task[0]](*task[1:])

        @block.vector
        def _(dve):
            steps = [0]

            def link(ins):
                steps[0] += 1
                ins.then_inc(dve_step, 1)
                dve.wait_ge(dve_step, steps[0])

            def convolve(q):
                cols = slice(q * PAIR * L, (q + 1) * PAIR * L)
                step_of = [0] * H
                for lag in range(1, DC):
                    for h in range(H):
                        ps = in_bank(q, h).rearrange("p (b l) -> p b l", b=PAIR)
                        acc = conv[:, h, cols].rearrange("p (b l) -> p b l", b=PAIR)
                        if lag == 1:
                            dve.wait_ge(tap_done, H * q + h + 1)
                        else:
                            dve.wait_ge(dve_step, step_of[h])
                        ins = nc.vector.scalar_tensor_tensor(
                            out=acc[:, :, lag:], in0=ps[:, :, :L - lag], scalar=v("conv_w", h * DC + DC - 1 - lag),
                            in1=acc[:, :, lag:], op0=ALU.mult, op1=ALU.add)
                        if lag < DC - 1:
                            steps[0] += 1
                            step_of[h] = steps[0]
                            ins.then_inc(dve_step, 1)
                        else:
                            ins.then_inc(conv_done, 1)

            def gate_of_z(b):
                dve.wait_ge(z_sigmoid, b + 1)
                nc.vector.tensor_tensor(gate_z[:, b % 2], z_norm[:], gate_z[:, b % 2], ALU.mult).then_inc(z_gated, 1)

            def z_moments(b):
                if b == 0:
                    dve.wait_ge(ld_x, 16)
                cols = slice(b * H, (b + 1) * H)
                for h in range(H):
                    last = nc.vector.bn_stats(stats[:, b * H + h, :], xs[:, b, h, :])
                link(last)
                for h in range(H):
                    last = nc.vector.bn_aggr(moments[:, b * H + h, :], stats[:, b * H + h, :])
                link(last)
                nc.vector.tensor_scalar(neg_mean[:, cols], moments[:, cols, 0], -1.0, None, ALU.mult)
                nc.vector.tensor_scalar(var_eps[:, cols], moments[:, cols, 1], EPS, None, ALU.add).then_inc(z_vars, 1)

            def delta(b):
                dve.wait_ge(sp_exped, b + 1)
                link(nc.vector.tensor_scalar(sp_rest[:], sp_exp[:], 1.0, -1.0, ALU.add, ALU.add))
                link(nc.vector.tensor_tensor(sp_fix[:], sp_exp[:], sp_rest[:], ALU.subtract))
                dve.wait_ge(sp_lned, b + 1)
                link(nc.vector.tensor_tensor(sp_rest[:], sp_ln[:], sp_fix[:], ALU.add))
                if b:
                    dve.wait_ge(rest_done, b)
                if b == 1:
                    dve.wait_ge(delta_ready, NU * DIRECT)
                link(nc.vector.tensor_tensor(vals[:, 0], sp_relu[:], sp_rest[:], ALU.add))
                dve.wait_ge(u_done, b + 1)
                link(nc.vector.tensor_tensor(vals[:, 1], vals[:, 0], u[:, b], ALU.mult))
                nc.vector.memset(vals[:, 0, :, 0:1], RESET).then_inc(vals_done, 1)

            def make_dbu(m):
                b = m // (NU * SB)
                dve.wait_ge(du_ready, m + 1)
                if m % (NU * SB) == 0:
                    await_read(dve, "b_rep", b)
                if m >= 3:
                    dve.wait_ge(scanned, m - 2)
                b_wide = b_rep[:, b % 3, :].rearrange("p (a l) -> p a l", a=1).broadcast_to([P, JB, L])
                nc.vector.tensor_tensor(dbu[:, m % 3, :].rearrange("p (j l) -> p j l", j=JB),
                                        du_ps[:, m % 2, :].rearrange("p (j l) -> p j l", j=JB), b_wide,
                                        ALU.mult).then_inc(dbu_done, 1)

            def scan(m):
                dve.wait_ge(dbu_done, m + 1)
                dve.wait_ge(da_ready, m + 1)
                if m % NU == 0 and m >= NU * RING:
                    dve.wait_ge(scaled, m // NU - RING + 1)
                cols = slice(m % NU * BANK, (m % NU + 1) * BANK)
                nc.vector.tensor_tensor_scan(state[:, m // NU % RING, cols], da[:, m % DA_RING, :], dbu[:, m % 3, :],
                                             0.0, ALU.mult, ALU.add).then_inc(scanned, 1)

            def gate(b):
                dve.wait_ge(summed, (b + 1) * SB)
                for h in range(H):
                    ins = nc.vector.scalar_tensor_tensor(out=yd[:, h, :], in0=u[:, b, h, :], scalar=v("d", h),
                                                         in1=y_ps[:, h, :], op0=ALU.mult, op1=ALU.add)
                ins.then_inc(y_read, 1)
                dve.wait_ge(y_read, b + 1)
                dve.wait_ge(z_gated, b + 1)
                nc.vector.tensor_tensor(yz[:], yd[:], gate_z[:, b % 2], ALU.mult).then_inc(yz_done, 1)

            def residual(b):
                for t in range(NT):
                    ps = await_slot(dve, "yt", b, t)
                    nc.vector.scalar_tensor_tensor(out=x1[:, b, t, :], in0=ps, scalar=tanh_g[:, 0:1],
                                                   in1=xs[:, b, t, :], op0=ALU.mult,
                                                   op1=ALU.add).then_inc(free_of("yt", b, t), 1)
                for t in range(NT):
                    await_read(dve, "yt", b, t)
                    last = nc.vector.bn_stats(stats2[:, b, t, :], x1[:, b, t, :])
                link(last)
                for t in range(NT):
                    last = nc.vector.bn_aggr(moments2[:, b, t, :], stats2[:, b, t, :])
                link(last)
                nc.vector.tensor_scalar(var_eps2[:, b, :], moments2[:, b, :, 1], EPS, None, ALU.add).then_inc(
                    x1_vars, 1)

            def normalize(b):
                dve.wait_ge(x1_rstd, b + 1)
                for t in range(NT):
                    if b:
                        await_read(dve, "xt", b - 1, t)
                    nc.vector.tensor_scalar(xn[:, t, :], x1[:, b, t, :], moments2[:, b, t, 0:1], rstd2[:, b, t:t + 1],
                                            ALU.subtract, ALU.mult).then_inc(xn_done, 1)

            def choose(b):
                ps = await_slot(dve, "logits", b)
                gate_b = v("gate_b").rearrange("p (a e) -> p a e", a=1).broadcast_to([P, NT, NE])
                nc.vector.tensor_tensor(logits[:], ps[:, 0:NT * NE].rearrange("p (t e) -> p t e", t=NT), gate_b,
                                        ALU.add).then_inc(free_of("logits", b), 1)
                await_read(dve, "logits", b)
                for t in range(NT):
                    last = nc.vector.max(top[:, t, :], logits[:, t, :])
                link(last)
                for t in range(NT):
                    last = nc.vector.max_index(top_at[:, t, :], top[:, t, :], logits[:, t, :])
                link(last)
                link(nc.vector.tensor_copy(top_f[:], top_at[:, :, 0:2]))
                iota = v("iota").rearrange("p (a e) -> p a e", a=1).broadcast_to([P, NT, NE])
                for m, place in ((mask0, 0), (mask1, 1)):
                    last = nc.vector.tensor_tensor(m[:], iota, top_f[:, :, place:place + 1].broadcast_to([P, NT, NE]),
                                                   ALU.is_equal)
                link(last)
                nc.vector.tensor_tensor(mask[:, b], mask0[:], mask1[:], ALU.add).then_inc(masks_done, 1)

            def fold_here(b, t):
                if b == NB - 1:
                    fold(dve, nc.vector, b, t)

            def combine(b, t):
                s = (b * NT + t) % 2
                for e in (NE - 2, NE - 1):
                    await_read(dve, "expert", b, t * NE + e)
                link(nc.vector.tensor_tensor(relus[:, s, 4 * DI:6 * DI], relus[:, s, 4 * DI:6 * DI],
                                             relus[:, s, 6 * DI:8 * DI], ALU.add))
                dve.wait_ge(folded, b * NT + t + 1)
                link(nc.vector.tensor_tensor(relus[:, s, 0:2 * DI], relus[:, s, 0:2 * DI],
                                             relus[:, s, 4 * DI:6 * DI], ALU.add))
                link(nc.vector.tensor_tensor(relus[:, s, 0:DI], relus[:, s, 0:DI], relus[:, s, DI:2 * DI], ALU.add))
                nc.vector.scalar_tensor_tensor(out=x1[:, b, t, :], in0=relus[:, s, 0:DI], scalar=half_tanh[:, 0:1],
                                               in1=x1[:, b, t, :], op0=ALU.mult, op1=ALU.add).then_inc(res_done, 1)

            run = {"z": gate_of_z, "z_moments": z_moments, "delta": delta, "gate": gate, "residual": residual, "normalize": normalize,
                   "choose": choose, "fold": fold_here,
                   "combine": combine}
            convolve(0)
            convolve(1)
            dve.wait_ge(a_exped, 1)
            nc.vector.tensor_scalar(a_neg[:], a_exp[:], A_LEAST, -1.0, ALU.max, ALU.mult).then_inc(a_made, 1)
            dve.wait_ge(tanh_done, 1)
            link(nc.vector.tensor_scalar(half_tanh[:], tanh_g[:, 1:2], 0.5, None, ALU.mult))
            delta(0)
            make_dbu(0)
            for i in range(STEPS):
                for n in range(NU):
                    if NU * i + n + 1 < NU * STEPS:
                        make_dbu(NU * i + n + 1)
                    scan(NU * i + n)
                    for task in SCHEDULE[NU * i + n]:
                        if task[0] in run:
                            run[task[0]](*task[1:])
            for task in SCHEDULE[NU * STEPS]:
                if task[0] in run:
                    run[task[0]](*task[1:])

        @block.tensor
        def _(pe):
            pe.wait_ge(ld_w, 16)
            for q in range(NB // PAIR):
                pe.wait_ge(ld_ctx[q], 16)
                for h in range(H):
                    nc.tensor.matmul(in_bank(q, h), w_in[:, h * P:(h + 1) * P],
                                     ctx[:, q * PAIR * L:(q + 1) * PAIR * L], start=True,
                                     stop=True).then_inc(in_ready, 1)

            def project_u(name, cols, b):
                pe.wait_ge(u_done, b + 1)
                ps = open_slot(pe, name, b)
                for h in range(H):
                    ins = nc.tensor.matmul(ps[0:cols.stop - cols.start, :], w_xp[:, h, cols], u[:, b, h, :],
                                           start=(h == 0), stop=(h == H - 1))
                ins.then_inc(work_ready, 1)

            def project_dt(h, b):
                await_read(pe, "dt_lo", b)
                ps = open_slot(pe, f"dt{h}", b)
                nc.tensor.matmul(ps, w_dt[:, h * P:(h + 1) * P], dt_lo[:, b % 2, :], start=True,
                                 stop=True).then_inc(work_ready, 1)

            def spread_into(m, bank, which):
                b, s = divmod(m // NU, SB)
                h, k = divmod(s, NK)
                j = m % NU * JB
                if m >= NU * DIRECT:
                    return nc.tensor.matmul(bank, spread[:, k, :], stack[:, b % 2, which, h * NJ + j:h * NJ + j + JB, :],
                                            start=True, stop=True)
                for n in range(JB):
                    ins = nc.tensor.matmul(bank[:, n * L:(n + 1) * L], direct[:, k, j + n, :], vals[:, which, h, :],
                                           start=True, stop=True)
                return ins

            def spread_unit(m):
                b = m // (NU * SB)
                if m == 0:
                    pe.wait_ge(ld_direct, 16)
                    pe.wait_ge(conv_done, H * NB // PAIR)
                    pe.wait_ge(vals_done, 1)
                if m == NU * DIRECT:
                    pe.wait_ge(ld_sel, 48)
                if m == (NU * SB * b if b else NU * DIRECT):
                    pe.wait_ge(turned_in, 16 * PARTS * (b + 1))
                if m >= 2:
                    pe.wait_ge(dbu_done, m - 1)
                spread_into(m, du_ps[:, m % 2, :], 1).then_inc(du_ready, 1)
                if m >= 2:
                    pe.wait_ge(da_ready, m - 1)
                spread_into(m, delta_ps[:, m % 2, :], 0).then_inc(delta_ready, 1)

            def sum_states(i):
                b, s = divmod(i, SB)
                h, k = divmod(s, NK)
                pe.wait_ge(scaled, i + 1)
                if s == 0 and b:
                    pe.wait_ge(y_read, b)
                for j in range(NJ):
                    ins = nc.tensor.matmul(y_ps[j * STRIP:(j + 1) * STRIP, h, :], gather[:, k, :],
                                           scaled_state[:, i % RING, j, :], start=(k == 0), stop=(k == NK - 1))
                ins.then_inc(summed, 1)

            def turn_y(b):
                pe.wait_ge(yz_done, b + 1)
                for t in range(NT):
                    ps = open_slot(pe, "yt", b, t)
                    for h in range(H):
                        ins = nc.tensor.transpose(ps[:, h * P:(h + 1) * P], yz[:, h, t * P:(t + 1) * P], ident[:])
                    ins.then_inc(work_ready, 1)

            def turn_xn(b):
                for t in range(NT):
                    pe.wait_ge(xn_done, b * NT + t + 1)
                    ps = open_slot(pe, "xt", b, t)
                    for k in range(2):
                        ins = nc.tensor.transpose(ps[:, k * P:(k + 1) * P], xn[:, t, k * P:(k + 1) * P], ident[:])
                    ins.then_inc(work_ready, 1)

            def choose(b):
                for t in range(NT):
                    await_read(pe, "xt", b, t)
                ps = open_slot(pe, "logits", b)
                gate_w = v("gate_w").rearrange("p (k e) -> p k e", k=2)
                for t in range(NT):
                    for k in range(2):
                        ins = nc.tensor.matmul(ps[:, t * NE:(t + 1) * NE], xnt[:, b, t, k, :], gate_w[:, k, :],
                                               start=(k == 0), stop=(k == 1))
                ins.then_inc(work_ready, 1)

            def expert(b, unit):
                t, e = divmod(unit, NE)
                cols = slice(e * DI, (e + 1) * DI)
                if b == 0 and unit == 0:
                    pe.wait_ge(ld_ew, 16)
                    pe.wait_ge(eb_moved, 16 * PARTS)
                    pe.wait_ge(ones_made, 1)
                ps = open_slot(pe, "expert", b, unit)
                nc.tensor.matmul(ps, ones[:], eb_rows[:, cols], start=True, stop=False)
                for k in range(2):
                    ins = nc.tensor.matmul(ps, xnt[:, b, t, k, :], ew[:, k, cols], start=False, stop=(k == 1))
                ins.then_inc(work_ready, 1)

            run = {"dt_lo": lambda b: project_u("dt_lo", slice(0, DR), b),
                   "b_rep": lambda b: project_u("b_rep", slice(DR, DR + P), b),
                   "c_rep": lambda b: project_u("c_rep", slice(DR + P, DR + 2 * P), b),
                   "dt0": lambda b: project_dt(0, b), "dt1": lambda b: project_dt(1, b),
                   "yt": turn_y, "xt": turn_xn, "logits": choose, "expert": expert}
            pe.wait_ge(ld_xp, 32)
            for name in FIRST:
                run[name](0)
            for m in range(PE_AHEAD):
                spread_unit(m)
            for i in range(STEPS):
                for n in range(NU):
                    if NU * i + n + PE_AHEAD < NU * STEPS:
                        spread_unit(NU * i + n + PE_AHEAD)
                    if n == 0 and i >= SUM_LAG:
                        sum_states(i - SUM_LAG)
                    for task in SCHEDULE[NU * i + n]:
                        if task[0] in run:
                            run[task[0]](*task[1:])
            for i in range(STEPS - SUM_LAG, STEPS):
                sum_states(i)
            for task in SCHEDULE[NU * STEPS]:
                if task[0] in run:
                    run[task[0]](*task[1:])


def kernel(x, ctx_1024, g_xattn, g_ffn, L0_xattn_in_proj_w, L0_xattn_conv_w, L0_xattn_conv_b, L0_xattn_x_proj_w,
           L0_xattn_dt_proj_w, L0_xattn_dt_proj_b, L0_xattn_A_log, L0_xattn_D, L0_ffn_gate_w, L0_ffn_gate_b,
           L0_ffn_expert_w, L0_ffn_expert_b):
    import numpy as np
    import ml_dtypes
    import concourse.bacc as bacc
    from concourse.bass_utils import run_bass_kernel_spmd

    def halves(a):
        a = np.asarray(a).reshape(H, P, -1)
        return a.transpose(1, 0, 2).reshape(P, -1)

    def rows(a):
        return np.broadcast_to(np.asarray(a).reshape(1, -1), (P, np.asarray(a).size))

    a_log = np.asarray(L0_xattn_A_log).reshape(H, NJ, NK, GC, NS).transpose(3, 4, 0, 2, 1).reshape(P, H * NK * NJ)
    vecs = np.concatenate([
        halves(L0_xattn_conv_w), halves(L0_xattn_conv_b), halves(L0_xattn_dt_proj_b), a_log, halves(L0_xattn_D),
        rows(g_xattn), rows(g_ffn), rows(L0_ffn_gate_b), halves(L0_ffn_gate_w),
        rows(np.arange(NE, dtype=np.float32)), rows(np.full(NB * H, -0.5, np.float32))], axis=1)
    choice = np.zeros((STRIP, NK, GC, NS), np.float32)
    for k in range(NK):
        for c in range(GC):
            choice[k * GC + c, k, c, :] = 1
    choice = choice.reshape(STRIP, NK, P)
    xp = np.asarray(L0_xattn_x_proj_w)
    xp = np.concatenate([xp[:DR], np.tile(xp[DR:DR + NS], (GC, 1)), np.tile(xp[DR + NS:], (GC, 1))], axis=0)
    arrays = {
        "ctxt": np.asarray(ctx_1024).transpose(2, 0, 1).reshape(DM, NB * L),
        "inpt": np.asarray(L0_xattn_in_proj_w).T,
        "xpt": xp.T.reshape(H, P, XD).transpose(1, 0, 2),
        "dtwt": np.asarray(L0_xattn_dt_proj_w).T,
        "vecs": vecs,
        "ident_in": np.eye(P, dtype=np.float32),
        "pick_in": np.tile(choice, (PARTS, 1, 1)).astype(ml_dtypes.bfloat16),
        "gather_in": choice.transpose(2, 1, 0),
        "direct_in": np.stack([np.pad(choice[:, :DIRECT], ((j * STRIP, P - (j + 1) * STRIP), (0, 0), (0, 0)))
                               for j in range(NJ)], axis=2),
        "x_in": np.asarray(x),
        "ew_in": np.asarray(L0_ffn_expert_w).reshape(NE, 2, P, DI).transpose(2, 1, 0, 3).reshape(P, 2, NE * DI),
        "eb_in": np.asarray(L0_ffn_expert_b).reshape(P, NE * DI // P),
    }
    arrays = {k: np.ascontiguousarray(a) for k, a in arrays.items()}
    nc = bacc.Bacc("TRN2", target_bir_lowering=False, num_devices=1)
    aps = {k: nc.dram_tensor(k, a.shape, mybir.dt.from_np(a.dtype), kind="ExternalInput").ap()
           for k, a in arrays.items()}
    out = nc.dram_tensor("out", (NB, L, DI), F32, kind="ExternalOutput").ap()
    flamingo_block(nc, **aps, out=out)
    return run_bass_kernel_spmd(nc, [arrays], core_ids=[0]).results[0]["out"]
```

```python
from contextlib import ExitStack

import concourse.bass as bass
from concourse import mybir

F32 = mybir.dt.float32
BF16 = mybir.dt.bfloat16
U32 = mybir.dt.uint32
ALU = mybir.AluOpType
ACT = mybir.ActivationFunctionType

P = 128
NB = 4
L = 256
DC = 4
DI = 256
DM = 128
NS = 16
DR = 8
NE = 8
H = DI // P
STRIP = 32
NJ = P // STRIP
GC = P // NS
NK = STRIP // GC
SB = H * NK
STEPS = NB * SB
NT = L // P
XD = DR + 2 * P
BANK = 512
JB = BANK // L
NU = NJ // JB
PARTS = 3
EPS = 1e-5
RESET = 1.0e30
A_LEAST = 1e-27
PAIR = 2
UNITS = NT * NE
WORK = 3
PE_AHEAD = 2
ACT_AHEAD = 2
DA_RING = 4
RING = 7
DIRECT = 2
SUM_LAG = 3

COLS = {}
_at = 0
for _name, _n in (("conv_w", H * DC), ("conv_b", H), ("dt_b", H), ("a_log", H * NK * NJ), ("d", H), ("g", 2),
                  ("gate_b", NE), ("gate_w", 2 * NE), ("iota", NE), ("power", NB * H)):
    COLS[_name] = slice(_at, _at + _n)
    _at += _n
NCOLS = _at


FIRST = (("dt_lo", 0), ("b_rep", 0), ("dt0", 0), ("dt1", 0), ("c_rep", 0), ("dt_lo", 1), ("b_rep", 1))
PREPARE = (("dt_lo", -26), ("b_rep", -25), ("c_rep", -24), ("dt0", -22), ("dt1", -22), ("soft", -20), ("delta", -19),
           ("high", -18), ("rest", -17), ("mid", -12), ("low", -9))
PREPARE_1 = (("c_rep", 0), ("dt0", 0), ("dt1", 0), ("soft", 0), ("delta", 3), ("high", 4), ("rest", 5), ("mid", 7),
             ("low", 8))
Z_AT = (("z_exp", 6), ("z", 13))
FINISH = (("gate", 4), ("yt", 5), ("residual", 5), ("normalize", 7), ("xt", 8), ("logits", 11), ("choose", 11))
UNITS_FROM = 12
UNITS_IN = 10
AHEAD = (("yt", 5), ("residual", 1), ("normalize", 3), ("xt", 0), ("logits", 2), ("choose", 1))


def extra(b, unit):
    tile, e = divmod(unit, NE)
    return {NE // 2 - 1: [("fold", b, tile)], NE - 1: [("combine", b, tile)]}.get(e, [])


def schedule():
    banks = NU * SB
    last = NB * banks
    at = [[] for _ in range(last + 1)]
    for b in range(NB):
        for name, bank in Z_AT:
            at[banks * b + bank].append((name, b))
    for b in range(1, NB):
        for name, bank in PREPARE_1 if b == 1 else PREPARE:
            at[(0 if b == 1 else banks * b) + bank].append((name, b))
    left = []
    for b in range(NB - 1):
        for name, bank in FINISH:
            at[banks * (b + 1) + bank].append((name, b))
        for unit in range(UNITS):
            here = [("expert", b, unit)] + extra(b, unit)
            bank = banks * (b + 1) + UNITS_FROM + unit * UNITS_IN // UNITS
            if bank < last:
                at[bank] += here
            else:
                left += here
    b = NB - 1
    tail = at[last]
    tail.append(("gate", b))
    for name, ahead in AHEAD:
        tail += left[:ahead] + [(name, b)]
        left = left[ahead:]
    tail += left
    for unit in range(UNITS):
        tail += [("expert", b, unit)] + extra(b, unit)
    return at


SCHEDULE = schedule()


def flamingo_block(nc, ctxt, inpt, xpt, dtwt, vecs, ident_in, pick_in, gather_in, direct_in, x_in, ew_in, eb_in, out):
    es = ExitStack()
    with es:
        def sb(name, shape, dt=F32):
            return es.enter_context(nc.sbuf_tensor(name, shape, dt))

        def pb(name, shape):
            return es.enter_context(nc.psum_tensor(name, shape, F32))

        def sem(name):
            return es.enter_context(nc.semaphore(name))

        turn = nc.dram_tensor("turn", (NB, PARTS, 2, H, P, L), BF16).ap()

        ctx = sb("ctx", [P, NB * L])
        w_in = sb("w_in", [P, DI])
        w_xp = sb("w_xp", [P, H, XD])
        w_dt = sb("w_dt", [DR, DI])
        vec = sb("vec", [P, NCOLS])
        ident = sb("ident", [P, P])
        spread = sb("spread", [PARTS * STRIP, NK, P], BF16)
        gather = sb("gather", [P, NK, STRIP])
        direct = sb("direct", [P, DIRECT, NJ, P])
        xs = sb("xs", [P, NB, H, L])
        ew = sb("ew", [P, 2, NE * DI])
        eb = sb("eb", [P, NE * DI // P])
        a_exp = sb("a_exp", [P, H * NK * NJ])
        a_neg = sb("a_neg", [P, H * NK * NJ])
        tanh_g = sb("tanh_g", [P, 2])
        half_tanh = sb("half_tanh", [P, 1])
        gate_z = sb("gate_z", [P, 2, H, L])
        z_norm = sb("z_norm", [P, H, L])
        stats = sb("stats", [P, NB * H, 6])
        moments = sb("moments", [P, NB * H, 2])
        var_eps = sb("var_eps", [P, NB * H])
        rstd = sb("rstd", [P, NB * H])
        neg_mean = sb("neg_mean", [P, NB * H])
        neg_mean_rstd = sb("neg_mean_rstd", [P, NB * H])
        ebp = sb("ebp", [P, PARTS, NE * DI // P], BF16)
        eb_rest = sb("eb_rest", [P, NE * DI // P])
        eb_rows = sb("eb_rows", [PARTS, NE * DI], BF16)
        ones = sb("ones", [PARTS, P], BF16)
        conv = sb("conv", [P, H, NB * L])
        u = sb("u", [P, NB, H, L])
        dt_lo = sb("dt_lo", [DR, 2, L])
        b_rep = sb("b_rep", [P, 3, L])
        c_rep = sb("c_rep", [P, 3, L])
        sp_abs = sb("sp_abs", [P, H, L])
        sp_relu = sb("sp_relu", [P, H, L])
        sp_exp = sb("sp_exp", [P, H, L])
        sp_ln = sb("sp_ln", [P, H, L])
        sp_rest = sb("sp_rest", [P, H, L])
        sp_fix = sb("sp_fix", [P, H, L])
        vals = sb("vals", [P, 2, H, L])
        vals_rest = sb("vals_rest", [P, 2, H, L])
        parts = sb("parts", [P, 2, PARTS, 2, H, L], BF16)
        stack = sb("stack", [PARTS * STRIP, 2, 2, H * NJ, L], BF16)
        da = sb("da", [P, DA_RING, BANK])
        dbu = sb("dbu", [P, 3, BANK])
        state = sb("state", [P, RING, NJ * L])
        yd = ctx[:, 0:H * L].rearrange("p (h l) -> p h l", h=H)
        yz = ctx[:, H * L:2 * H * L].rearrange("p (h l) -> p h l", h=H)
        x1 = sb("x1", [P, NB, NT, DI])
        stats2 = sb("stats2", [P, NB, NT, 6])
        moments2 = sb("moments2", [P, NB, NT, 2])
        var_eps2 = sb("var_eps2", [P, NB, NT])
        rstd2 = sb("rstd2", [P, NB, NT])
        xn = sb("xn", [P, NT, DI])
        xnt = sb("xnt", [P, NB, NT, 2, P])
        logits = sb("logits", [P, NT, NE])
        top = sb("top", [P, NT, 8])
        top_at = sb("top_at", [P, NT, 8], U32)
        top_f = sb("top_f", [P, NT, 2])
        mask0 = sb("mask0", [P, NT, NE])
        mask1 = sb("mask1", [P, NT, NE])
        mask = sb("mask", [P, NB, NT, NE])
        relus = sb("relus", [P, 2, NE * DI])

        delta_ps = pb("delta_ps", [P, 2, BANK])
        du_ps = pb("du_ps", [P, 2, BANK])
        y_ps = pb("y_ps", [P, H, L])
        work = pb("work", [P, WORK, BANK])

        ld_ctx = [sem(f"ld_ctx{q}") for q in range(NB // PAIR)]
        ld_w, ld_xp, ld_vec, ld_sel, ld_x = sem("ld_w"), sem("ld_xp"), sem("ld_vec"), sem("ld_sel"), sem("ld_x")
        ld_direct = sem("ld_direct")
        ld_eb, ld_ew, eb_moved = sem("ld_eb"), sem("ld_ew"), sem("eb_moved")
        turned_out = [sem(f"turned_out{part}") for part in range(PARTS)]
        turned_in = [sem(f"turned_in{n}") for n in range(H + NB - 1)]
        stored = sem("stored")
        ones_made, eb_split = sem("ones_made"), sem("eb_split")
        z_vars, z_rstd, z_bias = sem("z_vars"), sem("z_rstd"), sem("z_bias")
        z_normed, z_exped, z_lned = sem("z_normed"), sem("z_exped"), sem("z_lned")
        z_sigmoid, z_gated = sem("z_sigmoid"), sem("z_gated")
        tanh_done, a_exped, a_made = sem("tanh_done"), sem("a_exped"), sem("a_made")
        in_ready, tap_done, conv_done = sem("in_ready"), sem("tap_done"), sem("conv_done")
        u_done = sem("u_done")
        sp_abs_done, sp_exped, sp_lned = sem("sp_abs_done"), sem("sp_exped"), sem("sp_lned")
        vals_done, high_done, rest_done, mid_done, low_done = (
            sem("vals_done"), sem("high_done"), sem("rest_done"), sem("mid_done"), sem("low_done"))
        work_ready = sem("work_ready")
        work_free = [sem(f"work_free{s}") for s in range(WORK)]
        delta_ready, du_ready, dbu_done, da_ready = (
            sem("delta_ready"), sem("du_ready"), sem("dbu_done"), sem("da_ready"))
        scanned, scaled, summed, y_read = sem("scanned"), sem("scaled"), sem("summed"), sem("y_read")
        yz_done, x1_vars, x1_rstd, xn_done = sem("yz_done"), sem("x1_vars"), sem("x1_rstd"), sem("xn_done")
        masks_done, folded, res_done = sem("masks_done"), sem("folded"), sem("res_done")
        dve_step = sem("dve_step")

        def in_bank(q, h):
            return (delta_ps[:, 0, :], delta_ps[:, 1, :], du_ps[:, 0, :], du_ps[:, 1, :])[q * H + h]

        def v(name, i=None):
            s = vec[:, COLS[name]]
            return s if i is None else s[:, i:i + 1]

        all_tasks = list(FIRST)
        all_tasks += [task for tasks in SCHEDULE for task in tasks]
        order = {}

        def enlist(*item):
            order[item] = len(order)

        for task in all_tasks:
            kind, b = task[0], task[1]
            if kind in ("dt_lo", "b_rep", "c_rep", "dt0", "dt1"):
                enlist(kind, b)
            elif kind == "yt":
                for t in range(NT):
                    enlist("yt", b, t)
            elif kind == "xt":
                for t in range(NT):
                    enlist("xt", b, t)
            elif kind == "logits":
                enlist("logits", b)
            elif kind == "expert":
                enlist(*task)

        def open_slot(pe, *item):
            k = order[item]
            if k >= WORK:
                pe.wait_ge(work_free[k % WORK], k // WORK)
            return work[:, k % WORK, 0:L]

        def await_slot(eng, *item):
            eng.wait_ge(work_ready, order[item] + 1)
            return work[:, order[item] % WORK, 0:L]

        def await_read(eng, *item):
            k = order[item]
            eng.wait_ge(work_free[k % WORK], k // WORK + 1)

        def free_of(*item):
            return work_free[order[item] % WORK]

        def halves_of(b):
            return [slice(h, h + 1) for h in range(H)] if b == 0 else [slice(0, H)]

        def parcels(b, n=None):
            return (0 if b == 0 else H + b - 1) + (len(halves_of(b)) if n is None else n + 1)

        def fold(eng, alu, b, t):
            s = (b * NT + t) % 2
            for e in (NE // 2 - 2, NE // 2 - 1):
                await_read(eng, "expert", b, t * NE + e)
            alu.tensor_tensor(relus[:, s, 0:2 * DI], relus[:, s, 0:2 * DI], relus[:, s, 2 * DI:4 * DI],
                              ALU.add).then_inc(folded, 1)

        block = es.enter_context(nc.Block())

        @block.sync
        def _(sp):
            sp.dma_start(w_in[:], inpt).then_inc(ld_w, 16)
            for q in range(NB // PAIR):
                cols = slice(q * PAIR * L, (q + 1) * PAIR * L)
                sp.dma_start(ctx[:, cols], ctxt[:, cols]).then_inc(ld_ctx[q], 16)
            sp.dma_start(w_xp[:], xpt).then_inc(ld_xp, 16)
            sp.dma_start(w_dt[:], dtwt).then_inc(ld_xp, 16)
            sp.dma_start(spread[:], pick_in).then_inc(ld_sel, 16)
            sp.dma_start(gather[:], gather_in).then_inc(ld_sel, 16)
            sp.dma_start(direct[:], direct_in).then_inc(ld_direct, 16)
            sp.dma_start(ident[:], ident_in).then_inc(ld_sel, 16)

            def turn_parts(b):
                if b >= 2:
                    sp.wait_ge(delta_ready, NU * SB * (b - 1))
                    sp.wait_ge(du_ready, NU * SB * (b - 1))
                for n, hs in enumerate(halves_of(b)):
                    for part, done in enumerate((high_done, mid_done, low_done)):
                        sp.wait_ge(done, parcels(b, n))
                        sp.dma_start(turn[b, part, :, hs].rearrange("v h p l -> p v h l"),
                                     parts[:, b % 2, part, :, hs]).then_inc(turned_out[part], 16)
                        if part:
                            gather_part(b, n, hs, part - 1)
                    gather_part(b, n, hs, PARTS - 1)

            def gather_part(b, n, hs, part):
                sp.wait_ge(turned_out[part], 16 * parcels(b, n))
                for which in range(2):
                    source = turn[b, part, which, hs].rearrange("h (j c) l -> c (h j) l", c=STRIP)
                    groups = slice(hs.start * NJ, hs.stop * NJ)
                    sp.dma_start(stack[part * STRIP:(part + 1) * STRIP, b % 2, which, groups],
                                 source).then_inc(turned_in[parcels(b, n) - 1], 16)

            def store(b, t):
                sp.wait_ge(res_done, b * NT + t + 1)
                sp.dma_start(out[b, t * P:(t + 1) * P, :], x1[:, b, t, :]).then_inc(stored, 16)

            turn_parts(0)
            sp.dma_start(ew[:], ew_in).then_inc(ld_ew, 16)
            sp.wait_ge(eb_split, 5)
            for part in range(PARTS):
                sp.dma_start(eb_rows[part:part + 1, :], ebp[:, part, :]).then_inc(eb_moved, 16)
            for tasks in SCHEDULE:
                for task in tasks:
                    if task[0] == "low":
                        turn_parts(task[1])
                    if task[0] == "combine":
                        store(task[1], task[2])
            for arrived in turned_in:
                sp.wait_ge(arrived, 16 * PARTS * 2)
            sp.wait_ge(stored, 16 * NB * NT)

        @block.gpsimd
        def _(pool):
            nc.gpsimd.memset(ones[:], 1.0).then_inc(ones_made, 1)
            pool.wait_ge(ld_eb, 16)
            nc.gpsimd.tensor_copy(ebp[:, 0, :], eb[:]).then_inc(eb_split, 1)
            pool.wait_ge(eb_split, 1)
            nc.gpsimd.tensor_tensor(eb_rest[:], eb[:], ebp[:, 0, :], ALU.subtract).then_inc(eb_split, 1)
            pool.wait_ge(eb_split, 2)
            nc.gpsimd.tensor_copy(ebp[:, 1, :], eb_rest[:]).then_inc(eb_split, 1)
            pool.wait_ge(eb_split, 3)
            nc.gpsimd.tensor_tensor(eb[:], eb_rest[:], ebp[:, 1, :], ALU.subtract).then_inc(eb_split, 1)
            pool.wait_ge(eb_split, 4)
            nc.gpsimd.tensor_copy(ebp[:, 2, :], eb[:]).then_inc(eb_split, 1)
            pool.wait_ge(ld_vec, 16)

            pool.wait_ge(z_vars, 1)
            nc.gpsimd.tensor_tensor(rstd[:], var_eps[:], v("power"), ALU.pow).then_inc(z_rstd, 1)
            pool.wait_ge(z_rstd, 1)
            nc.gpsimd.tensor_tensor(neg_mean_rstd[:], neg_mean[:], rstd[:], ALU.mult).then_inc(z_bias, 1)

            def rest(b, n=0):
                hs = halves_of(b)[n]
                pool.wait_ge(high_done, parcels(b, n))
                if b:
                    pool.wait_ge(mid_done, parcels(b - 1))
                    pool.wait_ge(low_done, parcels(b - 1))
                nc.gpsimd.tensor_tensor(vals_rest[:, :, hs], vals[:, :, hs], parts[:, b % 2, 0, :, hs],
                                        ALU.subtract).then_inc(rest_done, 1)

            def low(b, n=0):
                hs = halves_of(b)[n]
                pool.wait_ge(mid_done, parcels(b, n))
                if b >= 2:
                    pool.wait_ge(turned_out[2], 16 * parcels(b - 2))
                nc.gpsimd.tensor_tensor(parts[:, b % 2, 2, :, hs], vals_rest[:, :, hs], parts[:, b % 2, 1, :, hs],
                                        ALU.subtract).then_inc(low_done, 1)

            def power(b):
                pool.wait_ge(x1_vars, b + 1)
                nc.gpsimd.tensor_tensor(rstd2[:, b, :], var_eps2[:, b, :], v("power")[:, 0:NT],
                                        ALU.pow).then_inc(x1_rstd, 1)

            def fold_here(b, t):
                if b < NB - 1:
                    fold(pool, nc.gpsimd, b, t)

            run = {"rest": rest, "low": low, "residual": power, "fold": fold_here}
            def scale_states(i):
                b = i // SB
                pool.wait_ge(scanned, NU * (i + 1))
                c_wide = c_rep[:, b % 3, :].rearrange("p (a l) -> p a l", a=1).broadcast_to([P, NJ, L])
                strips = state[:, i % RING, :].rearrange("p (j l) -> p j l", j=NJ)
                nc.gpsimd.tensor_tensor(strips, strips, c_wide,
                                        ALU.mult).then_inc(scaled, 1)

            for n in range(len(halves_of(0))):
                rest(0, n)
                low(0, n)
            for i in range(STEPS):
                if i < STEPS - 1:
                    scale_states(i)
                for task in SCHEDULE[NU * i] + SCHEDULE[NU * i + 1]:
                    if task[0] in run:
                        run[task[0]](*task[1:])
            for task in SCHEDULE[NU * STEPS]:
                if task[0] in run:
                    run[task[0]](*task[1:])

        @block.scalar
        def _(act):
            act.dma_start(vec[:], vecs).then_inc(ld_vec, 16)
            act.dma_start(xs[:], x_in.rearrange("b (h p) l -> p (b h) l", p=P)).then_inc(ld_x, 16)
            act.dma_start(eb[:], eb_in).then_inc(ld_eb, 16)

            nc.scalar.preload_act_table_set("silu_and_others")
            act.wait_ge(ld_vec, 16)
            nc.scalar.activation(tanh_g[:], v("g"), ACT.Tanh).then_inc(tanh_done, 1)

            for q in range(NB // PAIR):
                for h in range(H):
                    act.wait_ge(in_ready, H * q + h + 1)
                    nc.scalar.activation(conv[:, h, q * PAIR * L:(q + 1) * PAIR * L], in_bank(q, h), ACT.Identity,
                                         bias=v("conv_b", h), scale=v("conv_w", h * DC + DC - 1)).then_inc(tap_done, 1)

            def exp_delta(m):
                act.wait_ge(delta_ready, m + 1)
                if m >= DA_RING:
                    act.wait_ge(scanned, m - DA_RING + 1)
                for j in range(JB):
                    at = m % (NU * SB) * JB + j
                    cols = slice(j * L, (j + 1) * L)
                    ins = nc.scalar.activation(da[:, m % DA_RING, cols], delta_ps[:, m % 2, cols], ACT.Exp,
                                               scale=a_neg[:, at:at + 1])
                ins.then_inc(da_ready, 1)

            def activate_u(b):
                act.wait_ge(conv_done, H * (b // PAIR + 1))
                nc.scalar.activation(u[:, b], conv[:, :, b * L:(b + 1) * L], ACT.Silu).then_inc(u_done, 1)

            def exp_z(b):
                act.wait_ge(z_bias, 1)
                if b:
                    act.wait_ge(z_gated, b)
                if b >= 2:
                    act.wait_ge(yz_done, b - 1)
                for h in range(H):
                    t = b * H + h
                    ins = nc.scalar.activation(z_norm[:, h, :], xs[:, b, h, :], ACT.Identity, scale=rstd[:, t:t + 1],
                                               bias=neg_mean_rstd[:, t:t + 1])
                ins.then_inc(z_normed, 1)
                act.wait_ge(z_normed, b + 1)
                nc.scalar.activation(gate_z[:, b % 2], z_norm[:], ACT.Exp, scale=-1.0).then_inc(z_exped, 1)
                act.wait_ge(z_exped, b + 1)
                nc.scalar.activation(gate_z[:, b % 2], gate_z[:, b % 2], ACT.Ln, bias=1.0).then_inc(z_lned, 1)
                act.wait_ge(z_lned, b + 1)
                nc.scalar.activation(gate_z[:, b % 2], gate_z[:, b % 2], ACT.Exp, scale=-1.0).then_inc(z_sigmoid, 1)

            def copy_dt_lo(b):
                ps = await_slot(act, "dt_lo", b)
                nc.scalar.activation(dt_lo[:, b % 2, :], ps[0:DR, :], ACT.Copy).then_inc(free_of("dt_lo", b), 1)

            def copy_rep(name, rep, b):
                if b >= 3:
                    act.wait_ge(dbu_done, NU * SB * (b - 2))
                    act.wait_ge(scaled, SB * (b - 2))
                ps = await_slot(act, name, b)
                nc.scalar.activation(rep[:, b % 3, :], ps, ACT.Copy).then_inc(free_of(name, b), 1)

            def soften(h, b):
                ps = await_slot(act, f"dt{h}", b)
                if b:
                    act.wait_ge(vals_done, parcels(b - 1))
                nc.scalar.activation(sp_abs[:, h, :], ps, ACT.Abs, bias=v("dt_b", h)).then_inc(sp_abs_done, 1)
                nc.scalar.activation(sp_relu[:, h, :], ps, ACT.Relu, bias=v("dt_b", h)).then_inc(
                    free_of(f"dt{h}", b), 1)

            def soft(b):
                for n, hs in enumerate(halves_of(b)):
                    soften_exp(b, n, hs)

            def soften_exp(b, n, hs):
                act.wait_ge(sp_abs_done, H * b + hs.stop)
                nc.scalar.activation(sp_exp[:, hs], sp_abs[:, hs], ACT.Exp, scale=-1.0).then_inc(sp_exped, 1)
                act.wait_ge(sp_exped, parcels(b, n))
                nc.scalar.activation(sp_ln[:, hs], sp_exp[:, hs], ACT.Ln, bias=1.0).then_inc(sp_lned, 1)

            def high(b, n=0):
                hs = halves_of(b)[n]
                act.wait_ge(vals_done, parcels(b, n))
                if b >= 2:
                    act.wait_ge(turned_out[0], 16 * parcels(b - 2))
                nc.scalar.activation(parts[:, b % 2, 0, :, hs], vals[:, :, hs], ACT.Copy).then_inc(high_done, 1)

            def mid(b, n=0):
                hs = halves_of(b)[n]
                act.wait_ge(rest_done, parcels(b, n))
                if b >= 2:
                    act.wait_ge(turned_out[1], 16 * parcels(b - 2))
                nc.scalar.activation(parts[:, b % 2, 1, :, hs], vals_rest[:, :, hs], ACT.Copy).then_inc(mid_done, 1)

            def copy_xnt(b):
                for t in range(NT):
                    ps = await_slot(act, "xt", b, t)
                    nc.scalar.activation(xnt[:, b, t], ps.rearrange("p (k c) -> p k c", k=2), ACT.Copy).then_inc(
                        free_of("xt", b, t), 1)

            def expert(b, unit):
                tile, e = b * NT + unit // NE, unit % NE
                if e == 0:
                    act.wait_ge(masks_done, b + 1)
                    if tile >= 2:
                        act.wait_ge(res_done, tile - 1)
                ps = await_slot(act, "expert", b, unit)
                nc.scalar.activation(relus[:, tile % 2, e * DI:(e + 1) * DI], ps, ACT.Relu,
                                     scale=mask[:, b, unit // NE, e:e + 1]).then_inc(free_of("expert", b, unit), 1)

            run = {"z_exp": exp_z, "dt_lo": copy_dt_lo,
                   "b_rep": lambda b: copy_rep("b_rep", b_rep, b), "c_rep": lambda b: copy_rep("c_rep", c_rep, b),
                   "dt0": lambda b: soften(0, b), "dt1": lambda b: soften(1, b), "soft": soft, "high": high,
                   "mid": mid, "xt": copy_xnt, "expert": expert}
            activate_u(0)
            activate_u(1)
            run["dt_lo"](0)
            run["b_rep"](0)
            activate_u(2)
            activate_u(3)
            nc.scalar.preload_act_table_set("natural_log_exp_and_others")
            nc.scalar.activation(a_exp[:], v("a_log"), ACT.Exp).then_inc(a_exped, 1)
            for n, hs in enumerate(halves_of(0)):
                run[f"dt{n}"](0)
                soften_exp(0, n, hs)
            for name in ("c_rep",):
                run[name](0)
            act.wait_ge(a_made, 1)
            high(0, 0)
            run["dt_lo"](1)
            mid(0, 0)
            high(0, 1)
            exp_delta(0)
            run["b_rep"](1)
            mid(0, 1)
            for m in range(1, ACT_AHEAD):
                exp_delta(m)
            for i in range(STEPS):
                for n in range(NU):
                    if NU * i + n + ACT_AHEAD < NU * STEPS:
                        exp_delta(NU * i + n + ACT_AHEAD)
                    for task in SCHEDULE[NU * i + n]:
                        if task[0] in run:
                            run[task[0]](*task[1:])
            for task in SCHEDULE[NU * STEPS]:
                if task[0] in run:
                    run[task[0]](*task[1:])

        @block.vector
        def _(dve):
            steps = [0]

            def link(ins):
                steps[0] += 1
                ins.then_inc(dve_step, 1)
                dve.wait_ge(dve_step, steps[0])

            def convolve(q):
                cols = slice(q * PAIR * L, (q + 1) * PAIR * L)
                step_of = [0] * H
                for lag in range(1, DC):
                    for h in range(H):
                        ps = in_bank(q, h).rearrange("p (b l) -> p b l", b=PAIR)
                        acc = conv[:, h, cols].rearrange("p (b l) -> p b l", b=PAIR)
                        if lag == 1:
                            dve.wait_ge(tap_done, H * q + h + 1)
                        else:
                            dve.wait_ge(dve_step, step_of[h])
                        ins = nc.vector.scalar_tensor_tensor(
                            out=acc[:, :, lag:], in0=ps[:, :, :L - lag], scalar=v("conv_w", h * DC + DC - 1 - lag),
                            in1=acc[:, :, lag:], op0=ALU.mult, op1=ALU.add)
                        if lag < DC - 1:
                            steps[0] += 1
                            step_of[h] = steps[0]
                            ins.then_inc(dve_step, 1)
                        else:
                            ins.then_inc(conv_done, 1)

            def gate_of_z(b):
                dve.wait_ge(z_sigmoid, b + 1)
                nc.vector.tensor_tensor(gate_z[:, b % 2], z_norm[:], gate_z[:, b % 2], ALU.mult).then_inc(z_gated, 1)

            def delta(b):
                for n, hs in enumerate(halves_of(b)):
                    dve.wait_ge(sp_exped, parcels(b, n))
                    link(nc.vector.tensor_scalar(sp_rest[:, hs], sp_exp[:, hs], 1.0, -1.0, ALU.add, ALU.add))
                    link(nc.vector.tensor_tensor(sp_fix[:, hs], sp_exp[:, hs], sp_rest[:, hs], ALU.subtract))
                    dve.wait_ge(sp_lned, parcels(b, n))
                    link(nc.vector.tensor_tensor(sp_rest[:, hs], sp_ln[:, hs], sp_fix[:, hs], ALU.add))
                    if b:
                        dve.wait_ge(rest_done, parcels(b - 1))
                    if b == 1:
                        dve.wait_ge(delta_ready, NU * DIRECT)
                    link(nc.vector.tensor_tensor(vals[:, 0, hs], sp_relu[:, hs], sp_rest[:, hs], ALU.add))
                    dve.wait_ge(u_done, b + 1)
                    link(nc.vector.tensor_tensor(vals[:, 1, hs], vals[:, 0, hs], u[:, b, hs], ALU.mult))
                    nc.vector.memset(vals[:, 0, hs, 0:1], RESET).then_inc(vals_done, 1)

            def make_dbu(m):
                b = m // (NU * SB)
                dve.wait_ge(du_ready, m + 1)
                if m % (NU * SB) == 0:
                    await_read(dve, "b_rep", b)
                if m >= 3:
                    dve.wait_ge(scanned, m - 2)
                b_wide = b_rep[:, b % 3, :].rearrange("p (a l) -> p a l", a=1).broadcast_to([P, JB, L])
                nc.vector.tensor_tensor(dbu[:, m % 3, :].rearrange("p (j l) -> p j l", j=JB),
                                        du_ps[:, m % 2, :].rearrange("p (j l) -> p j l", j=JB), b_wide,
                                        ALU.mult).then_inc(dbu_done, 1)

            def scan(m):
                dve.wait_ge(dbu_done, m + 1)
                dve.wait_ge(da_ready, m + 1)
                if m % NU == 0 and m >= NU * RING:
                    dve.wait_ge(summed, m // NU - RING + 1)
                cols = slice(m % NU * BANK, (m % NU + 1) * BANK)
                nc.vector.tensor_tensor_scan(state[:, m // NU % RING, cols], da[:, m % DA_RING, :], dbu[:, m % 3, :],
                                             0.0, ALU.mult, ALU.add).then_inc(scanned, 1)

            def gate(b):
                dve.wait_ge(summed, (b + 1) * SB)
                for h in range(H):
                    ins = nc.vector.scalar_tensor_tensor(out=yd[:, h, :], in0=u[:, b, h, :], scalar=v("d", h),
                                                         in1=y_ps[:, h, :], op0=ALU.mult, op1=ALU.add)
                ins.then_inc(y_read, 1)
                dve.wait_ge(y_read, b + 1)
                dve.wait_ge(z_gated, b + 1)
                nc.vector.tensor_tensor(yz[:], yd[:], gate_z[:, b % 2], ALU.mult).then_inc(yz_done, 1)

            def residual(b):
                for t in range(NT):
                    ps = await_slot(dve, "yt", b, t)
                    nc.vector.scalar_tensor_tensor(out=x1[:, b, t, :], in0=ps, scalar=tanh_g[:, 0:1],
                                                   in1=xs[:, b, t, :], op0=ALU.mult,
                                                   op1=ALU.add).then_inc(free_of("yt", b, t), 1)
                for t in range(NT):
                    await_read(dve, "yt", b, t)
                    last = nc.vector.bn_stats(stats2[:, b, t, :], x1[:, b, t, :])
                link(last)
                for t in range(NT):
                    last = nc.vector.bn_aggr(moments2[:, b, t, :], stats2[:, b, t, :])
                link(last)
                nc.vector.tensor_scalar(var_eps2[:, b, :], moments2[:, b, :, 1], EPS, None, ALU.add).then_inc(
                    x1_vars, 1)

            def normalize(b):
                dve.wait_ge(x1_rstd, b + 1)
                for t in range(NT):
                    if b:
                        await_read(dve, "xt", b - 1, t)
                    nc.vector.tensor_scalar(xn[:, t, :], x1[:, b, t, :], moments2[:, b, t, 0:1], rstd2[:, b, t:t + 1],
                                            ALU.subtract, ALU.mult).then_inc(xn_done, 1)

            def choose(b):
                ps = await_slot(dve, "logits", b)
                gate_b = v("gate_b").rearrange("p (a e) -> p a e", a=1).broadcast_to([P, NT, NE])
                nc.vector.tensor_tensor(logits[:], ps[:, 0:NT * NE].rearrange("p (t e) -> p t e", t=NT), gate_b,
                                        ALU.add).then_inc(free_of("logits", b), 1)
                await_read(dve, "logits", b)
                for t in range(NT):
                    last = nc.vector.max(top[:, t, :], logits[:, t, :])
                link(last)
                for t in range(NT):
                    last = nc.vector.max_index(top_at[:, t, :], top[:, t, :], logits[:, t, :])
                link(last)
                link(nc.vector.tensor_copy(top_f[:], top_at[:, :, 0:2]))
                iota = v("iota").rearrange("p (a e) -> p a e", a=1).broadcast_to([P, NT, NE])
                for m, place in ((mask0, 0), (mask1, 1)):
                    last = nc.vector.tensor_tensor(m[:], iota, top_f[:, :, place:place + 1].broadcast_to([P, NT, NE]),
                                                   ALU.is_equal)
                link(last)
                nc.vector.tensor_tensor(mask[:, b], mask0[:], mask1[:], ALU.add).then_inc(masks_done, 1)

            def fold_here(b, t):
                if b == NB - 1:
                    fold(dve, nc.vector, b, t)

            def combine(b, t):
                s = (b * NT + t) % 2

                def relu(first, end):
                    return relus[:, s, first * DI:end * DI]

                def onto_x1(e):
                    return nc.vector.scalar_tensor_tensor(out=x1[:, b, t, :], in0=relu(e, e + 1),
                                                          scalar=half_tanh[:, 0:1], in1=x1[:, b, t, :],
                                                          op0=ALU.mult, op1=ALU.add)

                dve.wait_ge(folded, b * NT + t + 1)
                for e in (NE - 4, NE - 3):
                    await_read(dve, "expert", b, t * NE + e)
                link(nc.vector.tensor_tensor(relu(0, 2), relu(0, 2), relu(NE - 4, NE - 2), ALU.add))
                link(nc.vector.tensor_tensor(relu(0, 1), relu(0, 1), relu(1, 2), ALU.add))
                await_read(dve, "expert", b, t * NE + NE - 2)
                link(nc.vector.tensor_tensor(relu(0, 1), relu(0, 1), relu(NE - 2, NE - 1), ALU.add))
                link(onto_x1(0))
                await_read(dve, "expert", b, t * NE + NE - 1)
                onto_x1(NE - 1).then_inc(res_done, 1)

            run = {"z": gate_of_z, "delta": delta, "gate": gate, "residual": residual,
                   "normalize": normalize, "choose": choose, "fold": fold_here, "combine": combine}
            convolve(0)
            convolve(1)
            dve.wait_ge(ld_x, 16)
            for t in range(NB * H):
                last = nc.vector.bn_stats(stats[:, t, :], xs[:, t // H, t % H, :])
            link(last)
            for t in range(NB * H):
                last = nc.vector.bn_aggr(moments[:, t, :], stats[:, t, :])
            link(last)
            nc.vector.tensor_scalar(neg_mean[:], moments[:, :, 0], -1.0, None, ALU.mult)
            nc.vector.tensor_scalar(var_eps[:], moments[:, :, 1], EPS, None, ALU.add).then_inc(z_vars, 1)
            dve.wait_ge(a_exped, 1)
            nc.vector.tensor_scalar(a_neg[:], a_exp[:], A_LEAST, -1.0, ALU.max, ALU.mult).then_inc(a_made, 1)
            dve.wait_ge(tanh_done, 1)
            link(nc.vector.tensor_scalar(half_tanh[:], tanh_g[:, 1:2], 0.5, None, ALU.mult))
            delta(0)
            make_dbu(0)
            for i in range(STEPS):
                for n in range(NU):
                    if NU * i + n + 1 < NU * STEPS:
                        make_dbu(NU * i + n + 1)
                    scan(NU * i + n)
                    for task in SCHEDULE[NU * i + n]:
                        if task[0] in run:
                            run[task[0]](*task[1:])
            c_last = c_rep[:, (NB - 1) % 3, :].rearrange("p (a l) -> p a l", a=1).broadcast_to([P, NJ, L])
            await_read(dve, "c_rep", NB - 1)
            dve.wait_ge(scanned, NU * STEPS)
            dve.wait_ge(scaled, STEPS - 1)
            strips = state[:, (STEPS - 1) % RING, :].rearrange("p (j l) -> p j l", j=NJ)
            nc.vector.tensor_tensor(strips, strips, c_last,
                                    ALU.mult).then_inc(scaled, 1)
            for task in SCHEDULE[NU * STEPS]:
                if task[0] in run:
                    run[task[0]](*task[1:])

        @block.tensor
        def _(pe):
            pe.wait_ge(ld_w, 16)
            for q in range(NB // PAIR):
                pe.wait_ge(ld_ctx[q], 16)
                for h in range(H):
                    nc.tensor.matmul(in_bank(q, h), w_in[:, h * P:(h + 1) * P],
                                     ctx[:, q * PAIR * L:(q + 1) * PAIR * L], start=True,
                                     stop=True).then_inc(in_ready, 1)

            def project_u(name, cols, b):
                pe.wait_ge(u_done, b + 1)
                ps = open_slot(pe, name, b)
                for h in range(H):
                    ins = nc.tensor.matmul(ps[0:cols.stop - cols.start, :], w_xp[:, h, cols], u[:, b, h, :],
                                           start=(h == 0), stop=(h == H - 1))
                ins.then_inc(work_ready, 1)

            def project_dt(h, b):
                await_read(pe, "dt_lo", b)
                ps = open_slot(pe, f"dt{h}", b)
                nc.tensor.matmul(ps, w_dt[:, h * P:(h + 1) * P], dt_lo[:, b % 2, :], start=True,
                                 stop=True).then_inc(work_ready, 1)

            def spread_into(m, bank, which):
                b, s = divmod(m // NU, SB)
                h, k = divmod(s, NK)
                j = m % NU * JB
                if m >= NU * DIRECT:
                    strips = slice(h * NJ + j, h * NJ + j + JB)
                    return nc.tensor.matmul(bank, spread[:, k, :], stack[:, b % 2, which, strips, :], start=True,
                                            stop=True)
                for n in range(JB):
                    ins = nc.tensor.matmul(bank[:, n * L:(n + 1) * L], direct[:, k, j + n, :], vals[:, which, h, :],
                                           start=True, stop=True)
                return ins

            def spread_unit(m):
                b = m // (NU * SB)
                if m == 0:
                    pe.wait_ge(ld_direct, 16)
                    pe.wait_ge(conv_done, H * NB // PAIR)
                    pe.wait_ge(vals_done, 1)
                if m == NU * DIRECT:
                    pe.wait_ge(ld_sel, 48)
                if m == NU * DIRECT:
                    pe.wait_ge(turned_in[0], 16 * PARTS * 2)
                if m == NU * NK or b and m == NU * SB * b:
                    pe.wait_ge(turned_in[parcels(b) - 1], 16 * PARTS * 2)
                if m >= 2:
                    pe.wait_ge(dbu_done, m - 1)
                spread_into(m, du_ps[:, m % 2, :], 1).then_inc(du_ready, 1)
                if m >= 2:
                    pe.wait_ge(da_ready, m - 1)
                spread_into(m, delta_ps[:, m % 2, :], 0).then_inc(delta_ready, 1)

            def sum_states(i):
                b, s = divmod(i, SB)
                h, k = divmod(s, NK)
                pe.wait_ge(scaled, i + 1)
                if s == 0 and b:
                    pe.wait_ge(y_read, b)
                for j in range(NJ):
                    ins = nc.tensor.matmul(y_ps[j * STRIP:(j + 1) * STRIP, h, :], gather[:, k, :],
                                           state[:, i % RING, j * L:(j + 1) * L], start=(k == 0), stop=(k == NK - 1))
                ins.then_inc(summed, 1)

            def turn_y(b):
                pe.wait_ge(yz_done, b + 1)
                for t in range(NT):
                    ps = open_slot(pe, "yt", b, t)
                    for h in range(H):
                        ins = nc.tensor.transpose(ps[:, h * P:(h + 1) * P], yz[:, h, t * P:(t + 1) * P], ident[:])
                    ins.then_inc(work_ready, 1)

            def turn_xn(b):
                for t in range(NT):
                    pe.wait_ge(xn_done, b * NT + t + 1)
                    ps = open_slot(pe, "xt", b, t)
                    for k in range(2):
                        ins = nc.tensor.transpose(ps[:, k * P:(k + 1) * P], xn[:, t, k * P:(k + 1) * P], ident[:])
                    ins.then_inc(work_ready, 1)

            def choose(b):
                for t in range(NT):
                    await_read(pe, "xt", b, t)
                ps = open_slot(pe, "logits", b)
                gate_w = v("gate_w").rearrange("p (k e) -> p k e", k=2)
                for t in range(NT):
                    for k in range(2):
                        ins = nc.tensor.matmul(ps[:, t * NE:(t + 1) * NE], xnt[:, b, t, k, :], gate_w[:, k, :],
                                               start=(k == 0), stop=(k == 1))
                ins.then_inc(work_ready, 1)

            def expert(b, unit):
                t, e = divmod(unit, NE)
                cols = slice(e * DI, (e + 1) * DI)
                if b == 0 and unit == 0:
                    pe.wait_ge(ld_ew, 16)
                    pe.wait_ge(eb_moved, 16 * PARTS)
                    pe.wait_ge(ones_made, 1)
                ps = open_slot(pe, "expert", b, unit)
                nc.tensor.matmul(ps, ones[:], eb_rows[:, cols], start=True, stop=False)
                for k in range(2):
                    ins = nc.tensor.matmul(ps, xnt[:, b, t, k, :], ew[:, k, cols], start=False, stop=(k == 1))
                ins.then_inc(work_ready, 1)

            run = {"dt_lo": lambda b: project_u("dt_lo", slice(0, DR), b),
                   "b_rep": lambda b: project_u("b_rep", slice(DR, DR + P), b),
                   "c_rep": lambda b: project_u("c_rep", slice(DR + P, DR + 2 * P), b),
                   "dt0": lambda b: project_dt(0, b), "dt1": lambda b: project_dt(1, b),
                   "yt": turn_y, "xt": turn_xn, "logits": choose, "expert": expert}
            pe.wait_ge(ld_xp, 32)
            for name, b in FIRST:
                run[name](b)
            for m in range(PE_AHEAD):
                spread_unit(m)
            for i in range(STEPS):
                for n in range(NU):
                    if NU * i + n + PE_AHEAD < NU * STEPS:
                        spread_unit(NU * i + n + PE_AHEAD)
                    if n == 0 and i >= SUM_LAG:
                        sum_states(i - SUM_LAG)
                    for task in SCHEDULE[NU * i + n]:
                        if task[0] in run:
                            run[task[0]](*task[1:])
            for i in range(STEPS - SUM_LAG, STEPS):
                sum_states(i)
            for task in SCHEDULE[NU * STEPS]:
                if task[0] in run:
                    run[task[0]](*task[1:])


def kernel(x, ctx_1024, g_xattn, g_ffn, L0_xattn_in_proj_w, L0_xattn_conv_w, L0_xattn_conv_b, L0_xattn_x_proj_w,
           L0_xattn_dt_proj_w, L0_xattn_dt_proj_b, L0_xattn_A_log, L0_xattn_D, L0_ffn_gate_w, L0_ffn_gate_b,
           L0_ffn_expert_w, L0_ffn_expert_b):
    import numpy as np
    import ml_dtypes
    import concourse.bacc as bacc
    from concourse.bass_utils import run_bass_kernel_spmd

    def halves(a):
        a = np.asarray(a).reshape(H, P, -1)
        return a.transpose(1, 0, 2).reshape(P, -1)

    def rows(a):
        return np.broadcast_to(np.asarray(a).reshape(1, -1), (P, np.asarray(a).size))

    a_log = np.asarray(L0_xattn_A_log).reshape(H, NJ, NK, GC, NS).transpose(3, 4, 0, 2, 1).reshape(P, H * NK * NJ)
    vecs = np.concatenate([
        halves(L0_xattn_conv_w), halves(L0_xattn_conv_b), halves(L0_xattn_dt_proj_b), a_log, halves(L0_xattn_D),
        rows(g_xattn), rows(g_ffn), rows(L0_ffn_gate_b), halves(L0_ffn_gate_w),
        rows(np.arange(NE, dtype=np.float32)), rows(np.full(NB * H, -0.5, np.float32))], axis=1)
    choice = np.zeros((STRIP, NK, GC, NS), np.float32)
    for k in range(NK):
        for c in range(GC):
            choice[k * GC + c, k, c, :] = 1
    choice = choice.reshape(STRIP, NK, P)
    xp = np.asarray(L0_xattn_x_proj_w)
    xp = np.concatenate([xp[:DR], np.tile(xp[DR:DR + NS], (GC, 1)), np.tile(xp[DR + NS:], (GC, 1))], axis=0)
    arrays = {
        "ctxt": np.asarray(ctx_1024).transpose(2, 0, 1).reshape(DM, NB * L),
        "inpt": np.asarray(L0_xattn_in_proj_w).T,
        "xpt": xp.T.reshape(H, P, XD).transpose(1, 0, 2),
        "dtwt": np.asarray(L0_xattn_dt_proj_w).T,
        "vecs": vecs,
        "ident_in": np.eye(P, dtype=np.float32),
        "pick_in": np.tile(choice, (PARTS, 1, 1)).astype(ml_dtypes.bfloat16),
        "gather_in": choice.transpose(2, 1, 0),
        "direct_in": np.stack([np.pad(choice[:, :DIRECT], ((j * STRIP, P - (j + 1) * STRIP), (0, 0), (0, 0)))
                               for j in range(NJ)], axis=2),
        "x_in": np.asarray(x),
        "ew_in": np.asarray(L0_ffn_expert_w).reshape(NE, 2, P, DI).transpose(2, 1, 0, 3).reshape(P, 2, NE * DI),
        "eb_in": np.asarray(L0_ffn_expert_b).reshape(P, NE * DI // P),
    }
    arrays = {k: np.ascontiguousarray(a) for k, a in arrays.items()}
    nc = bacc.Bacc("TRN2", target_bir_lowering=False, num_devices=1)
    aps = {k: nc.dram_tensor(k, a.shape, mybir.dt.from_np(a.dtype), kind="ExternalInput").ap()
           for k, a in arrays.items()}
    out = nc.dram_tensor("out", (NB, L, DI), F32, kind="ExternalOutput").ap()
    flamingo_block(nc, **aps, out=out)
    return run_bass_kernel_spmd(nc, [arrays], core_ids=[0]).results[0]["out"]
```
